# Optimizing a Trainium2 kernel written in Bass

```python
import numpy as np
import jax
import jax.numpy as jnp

def _softmax(x, axis=-1):
    return jax.nn.softmax(x, axis=axis)

def _gelu(x):
    return jax.nn.gelu(x, approximate=True)

def _silu(x):
    return jax.nn.silu(x)

def _sigmoid(x):
    return jax.nn.sigmoid(x)

def _layernorm(x, axis=-1, eps=1e-05):
    m = jnp.mean(x, axis=axis, keepdims=True)
    v = jnp.var(x, axis=axis, keepdims=True)
    return (x - m) / jnp.sqrt(v + eps)

def _scatter_add(tgt, idx, src, axis=0):
    return tgt.at[idx].add(src)

def _segment_sum(src, seg, n):
    return jax.ops.segment_sum(src, seg, n)
kernel_name = 'mk_seq_postln_d4_jaxref_r8_21823c'

def setup_inputs(seed: int=0):
    np.random.seed(seed)
    _w = jnp.asarray

    def _L0_attn_setup():
        import jax, jax.numpy as jnp
        import numpy as np
        DIM = 256
        NUM_HEADS = 16
        HEAD_DIM = 128
        key = jax.random.key(seed)
        ks = jax.random.split(key, 9)
        B, S = (2, 256)
        s = lambda fan_in: 1.0 / np.sqrt(fan_in)
        return {'x': jax.random.normal(ks[0], (B, S, DIM), dtype=jnp.float32), 'Wq': jax.random.uniform(ks[1], (DIM, NUM_HEADS * HEAD_DIM), jnp.float32, -s(DIM), s(DIM)), 'bq': jax.random.uniform(ks[2], (NUM_HEADS * HEAD_DIM,), jnp.float32, -s(DIM), s(DIM)), 'Wk': jax.random.uniform(ks[3], (DIM, HEAD_DIM), jnp.float32, -s(DIM), s(DIM)), 'bk': jax.random.uniform(ks[4], (HEAD_DIM,), jnp.float32, -s(DIM), s(DIM)), 'Wv': jax.random.uniform(ks[5], (DIM, HEAD_DIM), jnp.float32, -s(DIM), s(DIM)), 'bv': jax.random.uniform(ks[6], (HEAD_DIM,), jnp.float32, -s(DIM), s(DIM)), 'Wo': jax.random.uniform(ks[7], (NUM_HEADS * HEAD_DIM, DIM), jnp.float32, -s(NUM_HEADS * HEAD_DIM), s(NUM_HEADS * HEAD_DIM)), 'bo': jax.random.uniform(ks[8], (DIM,), jnp.float32, -s(NUM_HEADS * HEAD_DIM), s(NUM_HEADS * HEAD_DIM))}
    _L0_attn_in = _L0_attn_setup()

    def _L0_ffn_setup():
        import jax, jax.numpy as jnp
        import numpy as np
        HIDDEN = 256
        INTER = 1024
        SCALE = 64.0

        def fwht(x):
            orig_shape = x.shape
            n = orig_shape[-1]
            x = x.reshape(-1, n)
            h = 1
            while h < n:
                x = x.reshape(-1, n // (2 * h), 2, h)
                a, b = (x[:, :, 0, :], x[:, :, 1, :])
                x = jnp.stack([a + b, a - b], axis=2).reshape(-1, n)
                h *= 2
            return (x / jnp.sqrt(jnp.asarray(n, x.dtype))).reshape(orig_shape)
        key = jax.random.key(seed)
        ks = jax.random.split(key, 8)
        inp = jax.random.normal(ks[0], (4, 256, HIDDEN), dtype=jnp.float32)
        SU_ug = jnp.where(jax.random.bernoulli(ks[1], 0.5, (HIDDEN,)), 1.0, -1.0).astype(jnp.float32)
        SU_dp = jnp.where(jax.random.bernoulli(ks[2], 0.5, (INTER,)), 1.0, -1.0).astype(jnp.float32)
        Wscale_ug = jax.random.uniform(ks[3], (2 * INTER,), jnp.float32, 0.5, 1.5)
        Wscale_dp = jax.random.uniform(ks[4], (HIDDEN,), jnp.float32, 0.5, 1.5)
        W_up = jax.random.normal(ks[5], (INTER, HIDDEN), dtype=jnp.float32) * 0.02
        W_gate = jax.random.normal(ks[6], (INTER, HIDDEN), dtype=jnp.float32) * 0.02
        W_down = jax.random.normal(ks[7], (HIDDEN, INTER), dtype=jnp.float32) * 0.02
        return {'input': inp, 'SU_ug': SU_ug, 'SU_dp': SU_dp, 'Wscale_ug': Wscale_ug, 'Wscale_dp': Wscale_dp, 'W_up': W_up, 'W_gate': W_gate, 'W_down': W_down}
    _L0_ffn_in = _L0_ffn_setup()

    def _L1_attn_setup():
        import jax, jax.numpy as jnp
        import numpy as np
        import math
        EMBED_DIM = 256
        N_HEADS = 16
        HEAD_DIM = EMBED_DIM // N_HEADS
        THETA_BASE = 10000.0

        def _rope_freqs(seq_len):
            i = jnp.arange(HEAD_DIM // 2, dtype=jnp.float32)
            inv_freq = 1.0 / THETA_BASE ** (2.0 * i / HEAD_DIM)
            pos = jnp.arange(seq_len, dtype=jnp.float32)
            th = jnp.outer(pos, inv_freq)
            return (jnp.cos(th), jnp.sin(th))

        def _rope(t, cos, sin):
            b, h, s, d = t.shape
            tr = t.reshape(b, h, s, d // 2, 2)
            x0, x1 = (tr[..., 0], tr[..., 1])
            r0 = x0 * cos - x1 * sin
            r1 = x0 * sin + x1 * cos
            return jnp.stack([r0, r1], axis=-1).reshape(b, h, s, d)
        key = jax.random.key(seed)
        k1, k2, k3 = jax.random.split(key, 3)
        B, S = (2, 256)
        x = jax.random.normal(k1, (B, S, EMBED_DIM), jnp.float32)
        scale = EMBED_DIM ** (-0.5)
        Wqkv = jax.random.normal(k2, (EMBED_DIM, 3 * EMBED_DIM), jnp.float32) * scale
        Wo = jax.random.normal(k3, (EMBED_DIM, EMBED_DIM), jnp.float32) * scale
        return {'x': x, 'Wqkv': Wqkv, 'Wo': Wo}
    _L1_attn_in = _L1_attn_setup()

    def _L1_ffn_setup():
        import jax, jax.numpy as jnp
        import numpy as np
        D_MODEL = 256
        D_EXPERT = 1024
        EPS = 1e-08

        def ternary_quant(w):
            scale = jnp.mean(jnp.abs(w)) + EPS
            q = jnp.clip(jnp.round(w / scale), -1.0, 1.0) * scale
            return w + jax.lax.stop_gradient(q - w)
        key = jax.random.key(seed)
        k_x, k_up, k_gate, k_down = jax.random.split(key, 4)
        std_in = 1.0 / np.sqrt(D_MODEL)
        std_exp = 1.0 / np.sqrt(D_EXPERT)
        return {'x': jax.random.normal(k_x, (4, 256, D_MODEL), dtype=jnp.float32), 'W_up': jax.random.normal(k_up, (D_EXPERT, D_MODEL), dtype=jnp.float32) * std_in, 'W_gate': jax.random.normal(k_gate, (D_EXPERT, D_MODEL), dtype=jnp.float32) * std_in, 'W_down': jax.random.normal(k_down, (D_MODEL, D_EXPERT), dtype=jnp.float32) * std_exp}
    _L1_ffn_in = _L1_ffn_setup()

    def _L2_attn_setup():
        import jax, jax.numpy as jnp
        import numpy as np
        B, S, D = (2, 512, 256)
        H = 16
        DC = 64
        DKQV = 256
        DR = 128
        DCKV = 64
        DOUT = 256
        DH = DKQV // H
        DRH = DR // H
        SCALER = 1.0 / float(np.sqrt(DH + DRH))

        def _rope(x):
            dr = x.shape[-1]
            inv_freq = 1.0 / 10000.0 ** (jnp.arange(0, dr, 2, dtype=jnp.float32) / dr)
            t = jnp.arange(x.shape[1], dtype=jnp.float32)
            freqs = t[:, None] * inv_freq[None, :]
            emb = jnp.concatenate([freqs, freqs], axis=-1)[None, :, None, :]
            x1, x2 = jnp.split(x, 2, axis=-1)
            rot = jnp.concatenate([-x2, x1], axis=-1)
            return x * jnp.cos(emb) + rot * jnp.sin(emb)
        key = jax.random.key(seed)
        ks = jax.random.split(key, 20)

        def lin(k, din, dout):
            s = 1.0 / np.sqrt(din)
            kw, kb = jax.random.split(k)
            W = jax.random.uniform(kw, (din, dout), jnp.float32, -s, s)
            b = jax.random.uniform(kb, (dout,), jnp.float32, -s, s)
            return (W, b)
        h_t = jax.random.normal(ks[0], (B, S, D), jnp.float32)
        Wc, bc = lin(ks[1], D, DC)
        Wcq, bcq = lin(ks[2], DC, DKQV)
        Wqr, bqr = lin(ks[3], DC, DR)
        Wckv, bckv = lin(ks[4], D, DCKV)
        Wck, bck = lin(ks[5], DCKV, DKQV)
        Wkr, bkr = lin(ks[6], D, DR)
        Wv, bv = lin(ks[7], DCKV, DKQV)
        Wo, bo = lin(ks[8], DKQV, DOUT)
        return dict(h_t=h_t, Wc=Wc, bc=bc, Wcq=Wcq, bcq=bcq, Wqr=Wqr, bqr=bqr, Wckv=Wckv, bckv=bckv, Wck=Wck, bck=bck, Wkr=Wkr, bkr=bkr, Wv=Wv, bv=bv, Wo=Wo, bo=bo)
    _L2_attn_in = _L2_attn_setup()

    def _L2_ffn_setup():
        import jax, jax.numpy as jnp
        import numpy as np
        EPS = 1e-08

        def _quantize(w):
            gamma = jnp.mean(jnp.abs(w))
            return jnp.clip(jnp.round(w / (gamma + EPS)), -1.0, 1.0)

        def _bitlinear(x, w):
            return jnp.matmul(x, _quantize(w).T)
        key = jax.random.key(seed)
        k1, k2, k3, k4 = jax.random.split(key, 4)
        d, h = (256, 704)
        x = jax.random.normal(k1, (4, 256, d), dtype=jnp.float32)
        w1 = jax.random.normal(k2, (h, d), dtype=jnp.float32)
        w2 = jax.random.normal(k3, (h, d), dtype=jnp.float32)
        w3 = jax.random.normal(k4, (d, h), dtype=jnp.float32)
        return {'x': x, 'w1': w1, 'w2': w2, 'w3': w3}
    _L2_ffn_in = _L2_ffn_setup()

    def _L3_attn_setup():
        import jax, jax.numpy as jnp
        import numpy as np
        import math
        HIDDEN = 256
        N_HEADS = 32
        N_KV = 8
        HEAD_DIM = HIDDEN // N_HEADS
        THETA = 10000.0
        B, S = (2, 256)

        def rope_cos_sin(seq_len, dim, theta, dtype):
            inv_freq = 1.0 / theta ** (jnp.arange(0, dim, 2, dtype=jnp.float32) / dim)
            pos = jnp.arange(seq_len, dtype=jnp.float32)
            freqs = jnp.outer(pos, inv_freq)
            emb = jnp.concatenate([freqs, freqs], -1)
            return (jnp.cos(emb).astype(dtype), jnp.sin(emb).astype(dtype))

        def rotate_half(x):
            x1, x2 = jnp.split(x, 2, axis=-1)
            return jnp.concatenate([-x2, x1], axis=-1)

        def apply_rope(x, cos, sin):
            c = cos[None, :, None, :]
            s = sin[None, :, None, :]
            return x * c + rotate_half(x) * s
        key = jax.random.key(seed)
        ks = jax.random.split(key, 5)
        sc = 0.02
        return {'hidden_states': jax.random.normal(ks[0], (B, S, HIDDEN), jnp.float32), 'wq': jax.random.normal(ks[1], (HIDDEN, HIDDEN), jnp.float32) * sc, 'wk': jax.random.normal(ks[2], (N_KV * HEAD_DIM, HIDDEN), jnp.float32) * sc, 'wv': jax.random.normal(ks[3], (N_KV * HEAD_DIM, HIDDEN), jnp.float32) * sc, 'wo': jax.random.normal(ks[4], (HIDDEN, HIDDEN), jnp.float32) * sc}
    _L3_attn_in = _L3_attn_setup()

    def _L3_ffn_setup():
        import jax, jax.numpy as jnp
        import numpy as np
        HIDDEN = 256
        INTER = 688
        LUT_SIZE = 16

        def _ghost_linear(x, idx, lut):
            w = lut[idx]
            return jnp.einsum('bsh,oh->bso', x, w)
        key = jax.random.key(seed)
        k_x, k_lut, k_g, k_u, k_d = jax.random.split(key, 5)
        x = jax.random.normal(k_x, (2, 512, HIDDEN), dtype=jnp.float32)
        lut = jax.random.normal(k_lut, (LUT_SIZE,), dtype=jnp.float32) * 0.02
        gate_idx = jax.random.randint(k_g, (INTER, HIDDEN), 0, LUT_SIZE, dtype=jnp.int32)
        up_idx = jax.random.randint(k_u, (INTER, HIDDEN), 0, LUT_SIZE, dtype=jnp.int32)
        down_idx = jax.random.randint(k_d, (HIDDEN, INTER), 0, LUT_SIZE, dtype=jnp.int32)
        return {'x': x, 'lut': lut, 'gate_idx': gate_idx, 'up_idx': up_idx, 'down_idx': down_idx}
    _L3_ffn_in = _L3_ffn_setup()
    _d = {'L0_attn_x': _L0_attn_in['x'], 'L0_attn_Wq': _L0_attn_in['Wq'], 'L0_attn_bq': _L0_attn_in['bq'], 'L0_attn_Wk': _L0_attn_in['Wk'], 'L0_attn_bk': _L0_attn_in['bk'], 'L0_attn_Wv': _L0_attn_in['Wv'], 'L0_attn_bv': _L0_attn_in['bv'], 'L0_attn_Wo': _L0_attn_in['Wo'], 'L0_attn_bo': _L0_attn_in['bo'], 'L0_ffn_SU_ug': _L0_ffn_in['SU_ug'], 'L0_ffn_SU_dp': _L0_ffn_in['SU_dp'], 'L0_ffn_Wscale_ug': _L0_ffn_in['Wscale_ug'], 'L0_ffn_Wscale_dp': _L0_ffn_in['Wscale_dp'], 'L0_ffn_W_up': _L0_ffn_in['W_up'], 'L0_ffn_W_gate': _L0_ffn_in['W_gate'], 'L0_ffn_W_down': _L0_ffn_in['W_down'], 'L1_attn_Wqkv': _L1_attn_in['Wqkv'], 'L1_attn_Wo': _L1_attn_in['Wo'], 'L1_ffn_W_up': _L1_ffn_in['W_up'], 'L1_ffn_W_gate': _L1_ffn_in['W_gate'], 'L1_ffn_W_down': _L1_ffn_in['W_down'], 'L2_attn_Wc': _L2_attn_in['Wc'], 'L2_attn_bc': _L2_attn_in['bc'], 'L2_attn_Wcq': _L2_attn_in['Wcq'], 'L2_attn_bcq': _L2_attn_in['bcq'], 'L2_attn_Wqr': _L2_attn_in['Wqr'], 'L2_attn_bqr': _L2_attn_in['bqr'], 'L2_attn_Wckv': _L2_attn_in['Wckv'], 'L2_attn_bckv': _L2_attn_in['bckv'], 'L2_attn_Wck': _L2_attn_in['Wck'], 'L2_attn_bck': _L2_attn_in['bck'], 'L2_attn_Wkr': _L2_attn_in['Wkr'], 'L2_attn_bkr': _L2_attn_in['bkr'], 'L2_attn_Wv': _L2_attn_in['Wv'], 'L2_attn_bv': _L2_attn_in['bv'], 'L2_attn_Wo': _L2_attn_in['Wo'], 'L2_attn_bo': _L2_attn_in['bo'], 'L2_ffn_w1': _L2_ffn_in['w1'], 'L2_ffn_w2': _L2_ffn_in['w2'], 'L2_ffn_w3': _L2_ffn_in['w3'], 'L3_attn_wq': _L3_attn_in['wq'], 'L3_attn_wk': _L3_attn_in['wk'], 'L3_attn_wv': _L3_attn_in['wv'], 'L3_attn_wo': _L3_attn_in['wo'], 'L3_ffn_lut': _L3_ffn_in['lut'], 'L3_ffn_gate_idx': _L3_ffn_in['gate_idx'], 'L3_ffn_up_idx': _L3_ffn_in['up_idx'], 'L3_ffn_down_idx': _L3_ffn_in['down_idx']}
    _x0 = _d['L0_attn_x']
    _d['L0_attn_x'] = jax.random.normal(jax.random.fold_in(jax.random.key(seed), 1), (16, 256, 256), dtype=_x0.dtype)
    del _x0
    return _d

def reference(L0_attn_x, L0_attn_Wq, L0_attn_bq, L0_attn_Wk, L0_attn_bk, L0_attn_Wv, L0_attn_bv, L0_attn_Wo, L0_attn_bo, L0_ffn_SU_ug, L0_ffn_SU_dp, L0_ffn_Wscale_ug, L0_ffn_Wscale_dp, L0_ffn_W_up, L0_ffn_W_gate, L0_ffn_W_down, L1_attn_Wqkv, L1_attn_Wo, L1_ffn_W_up, L1_ffn_W_gate, L1_ffn_W_down, L2_attn_Wc, L2_attn_bc, L2_attn_Wcq, L2_attn_bcq, L2_attn_Wqr, L2_attn_bqr, L2_attn_Wckv, L2_attn_bckv, L2_attn_Wck, L2_attn_bck, L2_attn_Wkr, L2_attn_bkr, L2_attn_Wv, L2_attn_bv, L2_attn_Wo, L2_attn_bo, L2_ffn_w1, L2_ffn_w2, L2_ffn_w3, L3_attn_wq, L3_attn_wk, L3_attn_wv, L3_attn_wo, L3_ffn_lut, L3_ffn_gate_idx, L3_ffn_up_idx, L3_ffn_down_idx):

    def _L0_attn_ref(x, Wq, bq, Wk, bk, Wv, bv, Wo, bo):
        import jax, jax.numpy as jnp
        import numpy as np
        DIM = 256
        NUM_HEADS = 16
        HEAD_DIM = 128
        B, S, _ = x.shape
        H, D = (NUM_HEADS, HEAD_DIM)
        q = (x @ Wq + bq).reshape(B, S, H, D)
        k = x @ Wk + bk
        v = x @ Wv + bv
        scale = 1.0 / np.sqrt(D).astype(np.float32)
        scores = jnp.einsum('bnhd,bmd->bnhm', q, k) * scale
        attn = jax.nn.softmax(scores, axis=-1)
        out = jnp.einsum('bnhm,bmd->bnhd', attn, v)
        out = out.reshape(B, S, H * D)
        return out @ Wo + bo

    def _L0_ffn_ref(input, SU_ug, SU_dp, Wscale_ug, Wscale_dp, W_up, W_gate, W_down):
        import jax, jax.numpy as jnp
        import numpy as np
        HIDDEN = 256
        INTER = 1024
        SCALE = 64.0

        def fwht(x):
            orig_shape = x.shape
            n = orig_shape[-1]
            x = x.reshape(-1, n)
            h = 1
            while h < n:
                x = x.reshape(-1, n // (2 * h), 2, h)
                a, b = (x[:, :, 0, :], x[:, :, 1, :])
                x = jnp.stack([a + b, a - b], axis=2).reshape(-1, n)
                h *= 2
            return (x / jnp.sqrt(jnp.asarray(n, x.dtype))).reshape(orig_shape)
        n = SU_ug.shape[0]
        x = input.reshape(-1, n)
        x = fwht(x * SU_ug) / SCALE
        x_up = x @ W_up.T * (Wscale_ug[:INTER] * SCALE)
        x_gate = x @ W_gate.T * (Wscale_ug[INTER:] * SCALE)
        x = jax.nn.silu(x_gate) * x_up
        x = fwht(x * SU_dp) / SCALE
        x = x @ W_down.T * (Wscale_dp * SCALE)
        return x.reshape(input.shape)

    def _L1_attn_ref(x, Wqkv, Wo):
        import jax, jax.numpy as jnp
        import numpy as np
        import math
        EMBED_DIM = 256
        N_HEADS = 16
        HEAD_DIM = EMBED_DIM // N_HEADS
        THETA_BASE = 10000.0

        def _rope_freqs(seq_len):
            i = jnp.arange(HEAD_DIM // 2, dtype=jnp.float32)
            inv_freq = 1.0 / THETA_BASE ** (2.0 * i / HEAD_DIM)
            pos = jnp.arange(seq_len, dtype=jnp.float32)
            th = jnp.outer(pos, inv_freq)
            return (jnp.cos(th), jnp.sin(th))

        def _rope(t, cos, sin):
            b, h, s, d = t.shape
            tr = t.reshape(b, h, s, d // 2, 2)
            x0, x1 = (tr[..., 0], tr[..., 1])
            r0 = x0 * cos - x1 * sin
            r1 = x0 * sin + x1 * cos
            return jnp.stack([r0, r1], axis=-1).reshape(b, h, s, d)
        B, S, E = x.shape
        H, D = (N_HEADS, E // N_HEADS)
        qkv = x @ Wqkv
        q, k, v = jnp.split(qkv, 3, axis=-1)
        heads = lambda t: t.reshape(B, S, H, D).transpose(0, 2, 1, 3)
        q, k, v = (heads(q), heads(k), heads(v))
        cos, sin = _rope_freqs(S)
        q = _rope(q, cos, sin)
        k = _rope(k, cos, sin)
        scores = jnp.einsum('bhqd,bhkd->bhqk', q, k) / math.sqrt(D)
        causal = jnp.tril(jnp.ones((S, S), dtype=bool))
        scores = jnp.where(causal, scores, -jnp.inf)
        attn = jax.nn.softmax(scores, axis=-1)
        op = jnp.einsum('bhqk,bhkd->bhqd', attn, v)
        op = op.transpose(0, 2, 1, 3).reshape(B, S, E)
        return op @ Wo

    def _L1_ffn_ref(x, W_up, W_gate, W_down):
        import jax, jax.numpy as jnp
        import numpy as np
        D_MODEL = 256
        D_EXPERT = 1024
        EPS = 1e-08

        def ternary_quant(w):
            scale = jnp.mean(jnp.abs(w)) + EPS
            q = jnp.clip(jnp.round(w / scale), -1.0, 1.0) * scale
            return w + jax.lax.stop_gradient(q - w)
        wu = ternary_quant(W_up)
        wg = ternary_quant(W_gate)
        wd = ternary_quant(W_down)
        up = jnp.einsum('bsd,ed->bse', x, wu)
        gate = jnp.einsum('bsd,ed->bse', x, wg)
        hidden = jax.nn.silu(up) * gate
        return jnp.einsum('bse,de->bsd', hidden, wd)

    def _L2_attn_ref(h_t, Wc, bc, Wcq, bcq, Wqr, bqr, Wckv, bckv, Wck, bck, Wkr, bkr, Wv, bv, Wo, bo):
        import jax, jax.numpy as jnp
        import numpy as np
        B, S, D = (2, 512, 256)
        H = 16
        DC = 64
        DKQV = 256
        DR = 128
        DCKV = 64
        DOUT = 256
        DH = DKQV // H
        DRH = DR // H
        SCALER = 1.0 / float(np.sqrt(DH + DRH))

        def _rope(x):
            dr = x.shape[-1]
            inv_freq = 1.0 / 10000.0 ** (jnp.arange(0, dr, 2, dtype=jnp.float32) / dr)
            t = jnp.arange(x.shape[1], dtype=jnp.float32)
            freqs = t[:, None] * inv_freq[None, :]
            emb = jnp.concatenate([freqs, freqs], axis=-1)[None, :, None, :]
            x1, x2 = jnp.split(x, 2, axis=-1)
            rot = jnp.concatenate([-x2, x1], axis=-1)
            return x * jnp.cos(emb) + rot * jnp.sin(emb)
        b, s = (h_t.shape[0], h_t.shape[1])
        cq = h_t @ Wc + bc
        q = (cq @ Wcq + bcq).reshape(b, s, H, DH)
        qr = _rope((cq @ Wqr + bqr).reshape(b, s, H, DRH))
        q = jnp.concatenate([q, qr], axis=-1)
        ckv = h_t @ Wckv + bckv
        k = (ckv @ Wck + bck).reshape(b, s, H, DH)
        kr = _rope((h_t @ Wkr + bkr).reshape(b, s, H, DRH))
        k = jnp.concatenate([k, kr], axis=-1)
        v = (ckv @ Wv + bv).reshape(b, s, H, DH)
        scores = jnp.einsum('bsid,bsjd->bsij', q, k) * SCALER
        attn = jax.nn.softmax(scores, axis=-1)
        out = jnp.einsum('bsij,bsjd->bsid', attn, v).reshape(b, s, DKQV)
        return out @ Wo + bo

    def _L2_ffn_ref(x, w1, w2, w3):
        import jax, jax.numpy as jnp
        import numpy as np
        EPS = 1e-08

        def _quantize(w):
            gamma = jnp.mean(jnp.abs(w))
            return jnp.clip(jnp.round(w / (gamma + EPS)), -1.0, 1.0)

        def _bitlinear(x, w):
            return jnp.matmul(x, _quantize(w).T)
        x1 = _bitlinear(x, w1)
        x2 = _bitlinear(x, w2)
        hidden = jax.nn.sigmoid(x1) * x2
        return _bitlinear(hidden, w3)

    def _L3_attn_ref(hidden_states, wq, wk, wv, wo):
        import jax, jax.numpy as jnp
        import numpy as np
        import math
        HIDDEN = 256
        N_HEADS = 32
        N_KV = 8
        HEAD_DIM = HIDDEN // N_HEADS
        THETA = 10000.0
        B, S = (2, 256)

        def rope_cos_sin(seq_len, dim, theta, dtype):
            inv_freq = 1.0 / theta ** (jnp.arange(0, dim, 2, dtype=jnp.float32) / dim)
            pos = jnp.arange(seq_len, dtype=jnp.float32)
            freqs = jnp.outer(pos, inv_freq)
            emb = jnp.concatenate([freqs, freqs], -1)
            return (jnp.cos(emb).astype(dtype), jnp.sin(emb).astype(dtype))

        def rotate_half(x):
            x1, x2 = jnp.split(x, 2, axis=-1)
            return jnp.concatenate([-x2, x1], axis=-1)

        def apply_rope(x, cos, sin):
            c = cos[None, :, None, :]
            s = sin[None, :, None, :]
            return x * c + rotate_half(x) * s
        b, s, _ = hidden_states.shape
        scale = 1.0 / math.sqrt(HEAD_DIM)
        group = N_HEADS // N_KV
        q = (hidden_states @ wq.T).reshape(b, s, N_HEADS, HEAD_DIM)
        k = (hidden_states @ wk.T).reshape(b, s, N_KV, HEAD_DIM)
        v = (hidden_states @ wv.T).reshape(b, s, N_KV, HEAD_DIM)
        cos, sin = rope_cos_sin(s, HEAD_DIM, THETA, hidden_states.dtype)
        q = apply_rope(q, cos, sin)
        k = apply_rope(k, cos, sin)
        k = jnp.repeat(k, group, axis=2)
        v = jnp.repeat(v, group, axis=2)
        scores = jnp.einsum('bqhd,bkhd->bhqk', q, k) * scale
        attn = jax.nn.softmax(scores, axis=-1)
        out = jnp.einsum('bhqk,bkhd->bqhd', attn, v)
        out = out.reshape(b, s, HIDDEN)
        return out @ wo.T

    def _L3_ffn_ref(x, lut, gate_idx, up_idx, down_idx):
        import jax, jax.numpy as jnp
        import numpy as np
        HIDDEN = 256
        INTER = 688
        LUT_SIZE = 16

        def _ghost_linear(x, idx, lut):
            w = lut[idx]
            return jnp.einsum('bsh,oh->bso', x, w)
        gate = _ghost_linear(x, gate_idx, lut)
        up = _ghost_linear(x, up_idx, lut)
        h = jax.nn.silu(gate) * up
        return _ghost_linear(h, down_idx, lut)
    x = L0_attn_x
    x = _layernorm(x + _L0_attn_ref(x, L0_attn_Wq, L0_attn_bq, L0_attn_Wk, L0_attn_bk, L0_attn_Wv, L0_attn_bv, L0_attn_Wo, L0_attn_bo), axis=-1)
    x = _layernorm(x + _L0_ffn_ref(x, L0_ffn_SU_ug, L0_ffn_SU_dp, L0_ffn_Wscale_ug, L0_ffn_Wscale_dp, L0_ffn_W_up, L0_ffn_W_gate, L0_ffn_W_down), axis=-1)
    x = _layernorm(x + _L1_attn_ref(x, L1_attn_Wqkv, L1_attn_Wo), axis=-1)
    x = _layernorm(x + _L1_ffn_ref(x, L1_ffn_W_up, L1_ffn_W_gate, L1_ffn_W_down), axis=-1)
    x = _layernorm(x + _L2_attn_ref(x, L2_attn_Wc, L2_attn_bc, L2_attn_Wcq, L2_attn_bcq, L2_attn_Wqr, L2_attn_bqr, L2_attn_Wckv, L2_attn_bckv, L2_attn_Wck, L2_attn_bck, L2_attn_Wkr, L2_attn_bkr, L2_attn_Wv, L2_attn_bv, L2_attn_Wo, L2_attn_bo), axis=-1)
    x = _layernorm(x + _L2_ffn_ref(x, L2_ffn_w1, L2_ffn_w2, L2_ffn_w3), axis=-1)
    x = _layernorm(x + _L3_attn_ref(x, L3_attn_wq, L3_attn_wk, L3_attn_wv, L3_attn_wo), axis=-1)
    x = _layernorm(x + _L3_ffn_ref(x, L3_ffn_lut, L3_ffn_gate_idx, L3_ffn_up_idx, L3_ffn_down_idx), axis=-1)
    return x

_drawn_inputs = setup_inputs


def setup_inputs(seed=0):
    import zlib

    import numpy as np

    out = dict(_drawn_inputs(seed))
    spreads = {}
    factors = {'L0_attn_Wq': 3.19,
     'L0_attn_bq': 8.0,
     'L0_attn_Wk': 3.167,
     'L0_attn_bk': 8.0,
     'L0_ffn_Wscale_dp': 3.095,
     'L2_attn_Wc': 4.729,
     'L2_attn_bc': 8.0,
     'L2_attn_Wcq': 7.434,
     'L2_attn_bcq': 8.0,
     'L2_attn_Wqr': 6.162,
     'L2_attn_bqr': 8.0,
     'L2_attn_bckv': 8.0,
     'L2_attn_Wck': 7.381,
     'L2_attn_bck': 8.0,
     'L2_attn_Wkr': 6.012,
     'L2_attn_bkr': 8.0,
     'L3_attn_wq': 8.0,
     'L3_attn_wk': 8.0,
     'L3_attn_wv': 5.209,
     'L3_attn_wo': 5.232}
    for name, (base, spread) in spreads.items():
        noise = np.random.default_rng([zlib.crc32(name.encode()), seed]).standard_normal(out[name].shape)
        drawn = base * np.exp(spread * noise) if base else spread * noise
        out[name] = jnp.asarray(drawn.astype(out[name].dtype))
    for name, factor in factors.items():
        out[name] = (out[name] * factor).astype(out[name].dtype)
    return out
```

```python
from contextlib import ExitStack

import numpy as np

import concourse.bass as bass
import concourse.mybir as mybir
from concourse.alu_op_type import AluOpType as ALU

F32 = mybir.dt.float32
F32R = mybir.dt.float32r
BF16 = mybir.dt.bfloat16
I32 = mybir.dt.int32
ACT = mybir.ActivationFunctionType
AX = mybir.AxisListType

P = 128
SEQS = 16
TOK = 256
TILES = TOK // P
DIM = 256
DC = DIM // P
LN_EPS = 1e-5
HI, LO = 0, 1
MASKED = -1e30
QUANT_EPS = 1e-8


def wait(eng, sem, per, b, k):
    if not isinstance(b, int) or per * b + k > 0:
        eng.wait_ge(sem, per * b + k)


def over_sequences(eng, body):
    body(0, 0, True, False)
    body(1, 1, False, False)
    with eng.Fori(1, SEQS // 2 - 1) as pair:
        body(2 * pair, 0, False, False)
        body(2 * pair + 1, 1, False, False)
    body(SEQS - 2, 0, False, False)
    body(SEQS - 1, 1, False, True)


class Memory:

    def __init__(self, nc, ctx, name):
        self.nc, self.ctx, self.name, self.sems = nc, ctx, name, []

    def sb(self, name, shape, dt=F32):
        return self.ctx.enter_context(self.nc.sbuf_tensor(f"{self.name}_{name}", shape, dt))

    def ps(self, name, shape, dt=F32):
        return self.ctx.enter_context(self.nc.psum_tensor(f"{self.name}_{name}", shape, dt))

    def sem(self, name):
        if not self.sems:
            self.ctx.callback(self.clear_semaphores)
        self.sems.append(self.nc.alloc_semaphore(f"{self.name}_{name}"))
        return self.sems[-1]

    def clear_semaphores(self):
        self.nc.clear_and_free_semaphores(self.sems)
        self.nc.all_engine_barrier()


def f32(ap):
    return ap.bitcast(F32)



def split_weights(nc, name, pairs, plain=()):
    with ExitStack() as ctx:
        m = Memory(nc, ctx, name)
        widest = max([p[1].shape[1] for p in pairs], default=1)
        raw = m.sb("raw", [P, 2, widest])
        loaded = [m.sem("loaded0"), m.sem("loaded1")]
        plain_loaded = m.sem("plain_loaded")
        hi_done, lo_done = m.sem("hi_done"), m.sem("lo_done")
        block = ctx.enter_context(nc.Block())

        @block.sync
        def _(sp):
            for target, source in plain:
                sp.dma_start(target, source).then_inc(plain_loaded, 16)
            for i, (source, hi, lo, rows) in enumerate(pairs):
                if i >= 2:
                    sp.wait_ge(lo_done, i - 1)
                sp.dma_start(raw[0:rows, i % 2, 0:hi.shape[1]], source).then_inc(loaded[i % 2], 16)
            sp.wait_ge(plain_loaded, 16 * len(plain))

        @block.scalar
        def _(act):
            for i, (source, hi, lo, rows) in enumerate(pairs):
                act.wait_ge(loaded[i % 2], 16 * (i // 2 + 1))
                nc.scalar.copy(hi, raw[0:rows, i % 2, 0:hi.shape[1]]).then_inc(hi_done, 1)

        @block.vector
        def _(dve):
            for i, (source, hi, lo, rows) in enumerate(pairs):
                dve.wait_ge(hi_done, i + 1)
                dve.tensor_tensor(lo, raw[0:rows, i % 2, 0:hi.shape[1]], f32(hi), ALU.subtract).then_inc(lo_done, 1)
            dve.wait_ge(lo_done, len(pairs))



class Norm:

    def __init__(self, m, consts):
        self.z = m.sb("z", [P, 2, TILES, DIM])
        self.stats = m.sb("stats", [P, 2, TILES, 6])
        self.mean_var = m.sb("mean_var", [P, 2, TILES, 2])
        self.rstd = m.sb("rstd", [P, 2, TILES, 1])
        self.y = m.sb("y", [P, 2, TILES, DIM])
        self.minus_half = consts["minus_half"]
        self.eps = consts["eps"]
        self.z_ready, self.var_eps_ready = m.sem("z_ready"), m.sem("var_eps_ready")
        self.measured = m.sem("measured")
        self.rstd_ready, self.y_ready = m.sem("rstd_ready"), m.sem("y_ready")
        self.stored = [m.sem("stored0"), m.sem("stored1")]

    def add_and_measure(self, dve, b, par, sublayer_out, x_res, factor=None):
        wait(dve, self.y_ready, TILES, b, -TILES)
        if factor is None:
            dve.tensor_tensor(self.z[:, par], sublayer_out, x_res, ALU.add).then_inc(self.z_ready, 1)
        else:
            dve.scalar_tensor_tensor(out=self.z[:, par], in0=sublayer_out, scalar=factor, in1=x_res,
                                     op0=ALU.mult, op1=ALU.add).then_inc(self.z_ready, 1)
        dve.wait_ge(self.z_ready, b + 1)
        for t in range(TILES):
            dve.bn_stats(self.stats[:, par, t], self.z[:, par, t]).then_inc(self.measured, 1)
        dve.wait_ge(self.measured, 3 * TILES * b + TILES)
        for t in range(TILES):
            dve.bn_aggr(self.mean_var[:, par, t], self.stats[:, par, t]).then_inc(self.measured, 2)

    def invert_root(self, pool, b, par):
        pool.wait_ge(self.measured, 3 * TILES * (b + 1))
        rstd = self.rstd[:, par, :, 0]
        wait(pool, self.y_ready, TILES, b, -TILES)
        pool.tensor_tensor(rstd, self.mean_var[:, par, :, 1], self.eps, ALU.add).then_inc(self.var_eps_ready, 1)
        pool.wait_ge(self.var_eps_ready, b + 1)
        pool.tensor_tensor(rstd, rstd, self.minus_half, ALU.pow).then_inc(self.rstd_ready, 1)

    def normalise(self, dve, b, par):
        dve.wait_ge(self.rstd_ready, b + 1)
        wait(dve, self.stored[par], 8, b - par, 0)
        for t in range(TILES):
            dve.tensor_scalar(self.y[:, par, t], self.z[:, par, t], self.mean_var[:, par, t, 0:1], self.rstd[:, par, t],
                              ALU.subtract, ALU.mult).then_inc(self.y_ready, 1)

    def store(self, sp, b, par, target):
        sp.wait_ge(self.y_ready, TILES * b + TILES)
        sp.dma_start(target, self.y[:, par]).then_inc(self.stored[par], 16)

    def wait_all_stored(self, sp):
        for stored in self.stored:
            sp.wait_ge(stored, 16 * (SEQS // 2))



def of_chunk(scale, m):
    return scale[:, m:m + 1] if scale.shape[1] > 1 else scale[:]


def ffn_block(nc, name, x_from, x_to, consts, w, act_func, act_scale=None, mul_scale=None, down_scale=None):
    parts, M = w["act"].shape[1], w["down"].shape[2]
    products = [(wp, xp) for wp in range(parts) for xp in (HI, LO) if wp + xp < 2]
    BANKS = 4
    with ExitStack() as ctx:
        m_ = Memory(nc, ctx, name)
        x_in = m_.sb("x_in", [P, 2, TILES, DIM])
        x_res = m_.sb("x_res", [P, 2, TILES, DIM])
        xT = m_.sb("xT", [P, 2, 2, DC, TOK], F32R)
        acted = m_.sb("acted", [P, 2, TOK])
        h32 = m_.sb("h32", [P, 2, TOK])
        h = m_.sb("h", [P, 2, M, TOK], F32R)
        norm = Norm(m_, consts)
        pT = m_.ps("pT", [P, DC, TOK])
        pH = [m_.ps(f"pH{i}", [P, 2, TOK]) for i in range(BANKS)]
        pD = [m_.ps(f"pD{i}", [P, TILES, DIM]) for i in range(2)]
        x_loaded = [m_.sem("x_loaded0"), m_.sem("x_loaded1")]
        res_loaded = [m_.sem("res_loaded0"), m_.sem("res_loaded1")]
        x_turned, xT_hi, xT_lo = m_.sem("x_turned"), m_.sem("xT_hi"), m_.sem("xT_lo")
        sides_ready, acted_ready, h32_ready = m_.sem("sides_ready"), m_.sem("acted_ready"), m_.sem("h32_ready")
        h_hi, h_lo, down_done = m_.sem("h_hi"), m_.sem("h_lo"), m_.sem("down_done")
        block = ctx.enter_context(nc.Block())

        @block.sync
        def _(sp):
            def load(b, par):
                wait(sp, x_turned, 1, b, -1)
                sp.dma_start(x_in[:, par], x_from(b)).then_inc(x_loaded[par], 16)
                wait(sp, norm.z_ready, 1, b, -1)
                sp.dma_start(x_res[:, par], x_from(b)).then_inc(res_loaded[par], 16)

            def body(b, par, first, last):
                if not last:
                    load(b + 1, 1 - par)
                if not first:
                    norm.store(sp, b - 1, 1 - par, x_to(b - 1))

            load(0, 0)
            over_sequences(sp, body)
            norm.store(sp, SEQS - 1, 1, x_to(SEQS - 1))
            norm.wait_all_stored(sp)

        @block.tensor
        def _(pe):
            def turn_x(b, par):
                pe.wait_ge(x_loaded[par], 8 * (b - par) + 16)
                wait(pe, xT_lo, 1, b, 0)
                for c in range(DC):
                    for t in range(TILES):
                        last = pe.transpose(pT[:, c, t * P:(t + 1) * P], x_in[:, par, t, c * P:(c + 1) * P], consts["ident"])
                last.then_inc(x_turned, 1)

            def hidden_sides(b, par, m):
                if m == 0:
                    pe.wait_ge(xT_lo, b + 1)
                wait(pe, h32_ready, M, b, m + 1 - BANKS)
                bank = pH[(M * par + m) % BANKS]
                for side, weights in enumerate((w["act"], w["mul"])):
                    for c in range(DC):
                        for wp, xp in products:
                            last = pe.matmul(bank[:, side], weights[:, wp, c, m * P:(m + 1) * P], xT[:, par, xp, c],
                                             start=side == 0 and c == 0 and (wp, xp) == products[0],
                                             stop=c == DC - 1 and (wp, xp) == products[-1], skip_group_check=True)
                last.then_inc(sides_ready, 1)

            def down(b, par, m):
                pe.wait_ge(h_lo, M * b + m + 1)
                if m == 0:
                    wait(pe, norm.z_ready, 1, b, -1)
                for t in range(TILES):
                    for wp, hp in products:
                        last = pe.matmul(pD[par][:, t], h[:, hp, m, t * P:(t + 1) * P], w["down"][:, wp, m],
                                         start=m == 0 and t == 0 and (wp, hp) == products[0],
                                         stop=m == M - 1 and (wp, hp) == products[-1], skip_group_check=True)
                last.then_inc(down_done, 1)

            def body(b, par, first, last):
                for m in range(M):
                    hidden_sides(b, par, m)
                    if m >= 2:
                        down(b, par, m - 2)
                    elif not first:
                        down(b - 1, 1 - par, M - 2 + m)
                    if m == 3 and not last:
                        turn_x(b + 1, 1 - par)

            turn_x(0, 0)
            over_sequences(pe, body)
            down(SEQS - 1, 1, M - 2)
            down(SEQS - 1, 1, M - 1)

        @block.scalar
        def _(act):
            def xT_to_hi(b, par):
                act.wait_ge(x_turned, b + 1)
                nc.scalar.copy(xT[:, par, HI], pT[:]).then_inc(xT_hi, 1)

            def activate(b, par, m):
                act.wait_ge(sides_ready, M * b + m + 1)
                wait(act, h32_ready, M, b, m - 1)
                nc.scalar.activation(acted[:, m % 2], pH[(M * par + m) % BANKS][:, 0], act_func,
                                     scale=1.0 if act_scale is None else of_chunk(act_scale, m)).then_inc(acted_ready, 1)

            def h_to_hi(b, m):
                act.wait_ge(h32_ready, M * b + m + 1)
                wait(act, down_done, M, b, m + 1 - M)
                nc.scalar.copy(h[:, HI, m], h32[:, m % 2]).then_inc(h_hi, 1)

            def body(b, par, first, last):
                for m in range(M):
                    activate(b, par, m)
                    if m >= 1:
                        h_to_hi(b, m - 1)
                    elif not first:
                        h_to_hi(b - 1, M - 1)
                    if m == 4 and not last:
                        xT_to_hi(b + 1, 1 - par)

            xT_to_hi(0, 0)
            over_sequences(act, body)
            h_to_hi(SEQS - 1, M - 1)

        @block.vector
        def _(dve):
            def xT_to_lo(b, par):
                dve.wait_ge(xT_hi, b + 1)
                dve.tensor_tensor(xT[:, par, LO], pT[:], f32(xT[:, par, HI]), ALU.subtract).then_inc(xT_lo, 1)

            def multiply(b, par, m):
                dve.wait_ge(acted_ready, M * b + m + 1)
                wait(dve, h_lo, M, b, m - 1)
                side = pH[(M * par + m) % BANKS][:, 1]
                if mul_scale is None:
                    step = dve.tensor_tensor(h32[:, m % 2], side, acted[:, m % 2], ALU.mult)
                else:
                    step = dve.scalar_tensor_tensor(out=h32[:, m % 2], in0=side, scalar=of_chunk(mul_scale, m),
                                                    in1=acted[:, m % 2], op0=ALU.mult, op1=ALU.mult)
                step.then_inc(h32_ready, 1)

            def h_to_lo(b, m):
                dve.wait_ge(h_hi, M * b + m + 1)
                dve.tensor_tensor(h[:, LO, m], h32[:, m % 2], f32(h[:, HI, m]), ALU.subtract).then_inc(h_lo, 1)

            def measure(b, par):
                dve.wait_ge(down_done, M * b + M)
                dve.wait_ge(res_loaded[par], 8 * (b - par) + 16)
                norm.add_and_measure(dve, b, par, pD[par][:], x_res[:, par], down_scale)

            def body(b, par, first, last):
                for m in range(M):
                    multiply(b, par, m)
                    if m >= 1:
                        h_to_lo(b, m - 1)
                    elif not first:
                        h_to_lo(b - 1, M - 1)
                    if m == 2 and not first:
                        measure(b - 1, 1 - par)
                    if m == 4 and not first:
                        norm.normalise(dve, b - 1, 1 - par)
                    if m == M - 1 and not last:
                        xT_to_lo(b + 1, 1 - par)

            xT_to_lo(0, 0)
            over_sequences(dve, body)
            h_to_lo(SEQS - 1, M - 1)
            measure(SEQS - 1, 1)
            norm.normalise(dve, SEQS - 1, 1)

        @block.gpsimd
        def _(pool):
            over_sequences(pool, lambda b, par, first, last: norm.invert_root(pool, b, par))



def hadamard_fold(nc, name, sources, w, signs, hadamard, down_scale):
    names = list(sources)
    with ExitStack() as ctx:
        m = Memory(nc, ctx, name)
        H = m.sb("H", [P, 2, P])
        H_parts = m.sb("H_parts", [P, 2, P], F32R)
        raw = {n: m.sb(f"raw_{n}", list(sources[n].shape)) for n in names}
        plain = {n: m.sb(f"plain_{n}", [P, 2] + list(sources[n].shape[1:]), F32R) for n in names}
        bank = [m.ps(f"bank{i}", [P, 512]) for i in range(4)]
        loaded, down_scaled, H_ready, hi_ready, lo_ready = m.sem("loaded"), m.sem("down_scaled"), m.sem("H_ready"), m.sem("hi_ready"), m.sem("lo_ready")
        folded, folded_hi, folded_lo = m.sem("folded"), m.sem("folded_hi"), m.sem("folded_lo")
        steps = []
        for n in names:
            chunks, outputs = sources[n].shape[1:]
            for i in range(chunks):
                for first in range(0, outputs, 512):
                    steps.append((n, chunks, i, first, min(512, outputs - first)))
        block = ctx.enter_context(nc.Block())

        @block.sync
        def _(sp):
            sp.dma_start(H[:], hadamard).then_inc(loaded, 16)
            sp.wait_ge(loaded, 16)
            for k, n in enumerate(names):
                sp.dma_start(raw[n][:], sources[n]).then_inc(loaded, 16)
                sp.wait_ge(loaded, 16 * (k + 2))

        @block.scalar
        def _(act):
            act.wait_ge(loaded, 16)
            nc.scalar.copy(H_parts[:], H[:]).then_inc(H_ready, 1)
            for k, n in enumerate(names):
                act.wait_ge(loaded, 16 * (k + 2))
                if n == "down":
                    act.wait_ge(down_scaled, 1)
                nc.scalar.copy(plain[n][:, HI], raw[n][:]).then_inc(hi_ready, 1)
            for s, (n, chunks, i, first, count) in enumerate(steps):
                act.wait_ge(folded, s + 1)
                nc.scalar.activation(w[n][:, HI, i, first:first + count], bank[s % 4][:, 0:count], ACT.Identity,
                                     scale=signs[n][:, i:i + 1]).then_inc(folded_hi, 1)

        @block.tensor
        def _(pe):
            pe.wait_ge(H_ready, 1)
            for s, (n, chunks, i, first, count) in enumerate(steps):
                pe.wait_ge(lo_ready, names.index(n) + 1)
                if s >= 4:
                    pe.wait_ge(folded_lo, s - 3)
                for j in range(chunks):
                    sign = bin(i & j).count("1") % 2
                    for part in (HI, LO):
                        last = pe.matmul(bank[s % 4][:, 0:count], H_parts[:, sign], plain[n][:, part, j, first:first + count],
                                         start=j == 0 and part == HI, stop=j == chunks - 1 and part == LO)
                last.then_inc(folded, 1)

        @block.vector
        def _(dve):
            for k, n in enumerate(names):
                if n == "down":
                    dve.wait_ge(loaded, 16 * (k + 2))
                    scale = down_scale[:].unsqueeze(1).to_broadcast(list(raw[n].shape))
                    dve.tensor_tensor(raw[n][:], raw[n][:], scale, ALU.mult).then_inc(down_scaled, 1)
                dve.wait_ge(hi_ready, k + 1)
                dve.tensor_tensor(plain[n][:, LO], raw[n][:], f32(plain[n][:, HI]), ALU.subtract).then_inc(lo_ready, 1)
            for s, (n, chunks, i, first, count) in enumerate(steps):
                dve.wait_ge(folded_hi, s + 1)
                dve.scalar_tensor_tensor(out=w[n][:, LO, i, first:first + count], in0=bank[s % 4][:, 0:count],
                                         scalar=signs[n][:, i:i + 1], in1=f32(w[n][:, HI, i, first:first + count]),
                                         op0=ALU.mult, op1=ALU.subtract).then_inc(folded_lo, 1)
            dve.wait_ge(folded_lo, len(steps))


def ternary_weights(nc, name, sources, w, count, scales):
    names = list(sources)
    with ExitStack() as ctx:
        m = Memory(nc, ctx, name)
        raw = m.sb("raw", [P, len(names)] + [int(np.prod(sources[names[0]].shape[1:]))])
        below = m.sb("below", [P, len(names), raw.shape[2]])
        sums = m.sb("sums", [P, 4])
        ones = m.sb("ones", [P, P])
        half = m.sb("half", [P, 2, 4])
        total = m.ps("total", [P, 4])
        loaded = [m.sem(f"loaded_{n}") for n in names]
        set_up, summed, totalled = m.sem("set_up"), m.sem("summed"), m.sem("totalled")
        scaled, halved, compared, done = m.sem("scaled"), m.sem("halved"), m.sem("compared"), m.sem("done")
        block = ctx.enter_context(nc.Block())

        @block.sync
        def _(sp):
            for k, n in enumerate(names):
                sp.dma_start(raw[:, k], sources[n].rearrange("p a b -> p (a b)")).then_inc(loaded[k], 16)

        @block.tensor
        def _(pe):
            pe.wait_ge(set_up, 2)
            pe.wait_ge(summed, len(names))
            pe.matmul(total[:], ones[:], sums[:], start=True, stop=True).then_inc(totalled, 1)

        @block.vector
        def _(dve):
            dve.memset(ones[:], 1.0).then_inc(set_up, 1)
            dve.memset(sums[:], 0.0).then_inc(set_up, 1)
            dve.wait_ge(set_up, 2)
            for k, n in enumerate(names):
                dve.wait_ge(loaded[k], 16)
                dve.tensor_reduce(sums[:, k:k + 1], raw[:, k], AX.X, ALU.add, apply_absolute_value=True).then_inc(summed, 1)
            dve.wait_ge(totalled, 1)
            for k, n in enumerate(names):
                dve.tensor_scalar(scales[n], total[:, k:k + 1], 1.0 / count, QUANT_EPS, ALU.mult, ALU.add).then_inc(scaled, 1)
            dve.wait_ge(scaled, len(names))
            for k, n in enumerate(names):
                for sign, factor in ((0, 0.5), (1, -0.5)):
                    dve.tensor_scalar(half[:, sign, k:k + 1], scales[n], factor, None, ALU.mult).then_inc(halved, 1)
            dve.wait_ge(halved, 2 * len(names))
            for k, n in enumerate(names):
                dve.tensor_scalar(below[:, k], raw[:, k], half[:, 1, k:k + 1], None, ALU.is_lt).then_inc(compared, 1)
            for k, n in enumerate(names):
                dve.wait_ge(compared, k + 1)
                dve.scalar_tensor_tensor(out=w[n][:, 0].rearrange("p a b -> p (a b)"), in0=raw[:, k],
                                         scalar=half[:, 0, k:k + 1], in1=below[:, k], op0=ALU.is_gt,
                                         op1=ALU.subtract).then_inc(done, 1)
            dve.wait_ge(done, len(names))


def looked_up_weights(nc, name, sources, w, lut, lut_size):
    names = list(sources)
    adds = lut_size - 1
    with ExitStack() as ctx:
        m = Memory(nc, ctx, name)
        n_of = int(np.prod(sources[names[0]].shape[1:]))
        index_int = m.sb("index_int", [P, n_of], I32)
        index = m.sb("index", [P, n_of])
        entry = m.sb("entry", [P, 2, n_of])
        total = m.sb("total", [P, 2, n_of])
        loaded, cast, entry_ready, added = m.sem("loaded"), m.sem("cast"), m.sem("entry_ready"), m.sem("added")
        hi_ready, lo_ready = m.sem("hi_ready"), m.sem("lo_ready")
        block = ctx.enter_context(nc.Block())

        @block.sync
        def _(sp):
            for k, n in enumerate(names):
                if k:
                    sp.wait_ge(cast, k)
                sp.dma_start(index_int[:], sources[n].rearrange("p a b -> p (a b)")).then_inc(loaded, 16)

        @block.vector
        def _(dve):
            for k, n in enumerate(names):
                dve.wait_ge(loaded, 16 * (k + 1))
                if k:
                    dve.wait_ge(lo_ready, k)
                dve.tensor_copy(index[:], index_int[:]).then_inc(cast, 1)
                dve.wait_ge(cast, k + 1)
                for v in range(lut_size):
                    if v >= 3:
                        dve.wait_ge(added, adds * k + v - 2)
                    dve.tensor_scalar(entry[:, v % 2] if v else total[:, 0], index[:], float(v), lut[:, v:v + 1],
                                      ALU.is_equal, ALU.mult).then_inc(entry_ready, 1)
                    dve.wait_ge(entry_ready, lut_size * k + v + 1)
                    if v:
                        if v >= 2:
                            dve.wait_ge(added, adds * k + v - 1)
                        dve.tensor_tensor(total[:, v % 2], total[:, 1 - v % 2], entry[:, v % 2], ALU.add).then_inc(added, 1)
                dve.wait_ge(hi_ready, k + 1)
                dve.tensor_tensor(w[n][:, LO].rearrange("p a b -> p (a b)"), total[:, adds % 2],
                                  f32(w[n][:, HI].rearrange("p a b -> p (a b)")), ALU.subtract).then_inc(lo_ready, 1)
            dve.wait_ge(lo_ready, len(names))

        @block.scalar
        def _(act):
            for k, n in enumerate(names):
                act.wait_ge(added, adds * (k + 1))
                nc.scalar.copy(w[n][:, HI].rearrange("p a b -> p (a b)"), total[:, adds % 2]).then_inc(hi_ready, 1)



class Piece:

    def __init__(self, target, first_head, heads, dims, offset, source, plain, swapped=None, table=None, bias=None,
                 swapped_bias=None):
        self.target, self.first_head, self.heads, self.dims, self.offset = target, first_head, heads, dims, offset
        self.source, self.plain, self.swapped, self.table = source, plain, swapped, table
        self.bias, self.swapped_bias = bias, swapped_bias


GROUP = 8
QUAD = 32
PROBS = 4
GUARD_ROW = 96
VALUES_LAG, SCORES_LAG = 2, 3


def over_bodies(eng, body, ahead=1):
    for i in (-1, 0, 1, 2):
        body(i, i % 2)
    pairs = SEQS // 2 - ahead
    with eng.Fori(1, pairs) as pair:
        body(2 * pair + 1, 1)
        body(2 * pair + 2, 0)
    for i in range(2 * pairs + 1, SEQS + 2):
        body(i, i % 2)


def sequence_of(stage, i):
    b = i + {"A": 1, "M": 0, "B": -1, "C": -2, "N": -2}[stage]
    return b if not isinstance(b, int) or 0 <= b < SEQS else None


def small_attention_block(nc, name, x_from, x_to, consts, heads, kv_heads, head_dims, v_dims, scale, pieces, w,
                          causal=False, latent=None, v_bias=None, out_bias=None):
    NP, G, per_kv = len(pieces), heads // GROUP, heads // kv_heads
    rotated = [k for k, p in enumerate(pieces) if p.table is not None]
    plain = [k for k, p in enumerate(pieces) if p.table is None]
    v_features = kv_heads * v_dims
    v_source = "x" if latent is None else "latent"
    out_features = heads * v_dims
    assert out_features == DIM and 3 * head_dims <= GUARD_ROW

    def last_head(piece):
        per = 1 if piece.target == "q" else per_kv
        return (piece.first_head + piece.heads) * per

    def serves_first(piece, h):
        return h == piece.first_head * (1 if piece.target == "q" else per_kv)

    scores_lag = 0
    ends = [last_head(p) for p in pieces]
    piece_slot = [end + (1 if end == heads else 2) * ends[:k].count(end) for k, end in enumerate(ends)]
    schedule = []
    for s in range(heads + SCORES_LAG + 1):
        if s < heads:
            schedule.append(("B", "scoresT", s))
        if 0 <= s - scores_lag < heads:
            schedule.append(("M", "scores", s - scores_lag))
        if s - scores_lag == heads:
            schedule.append(("M", "turn_max", 0))
        if 0 <= s - VALUES_LAG < heads:
            schedule.append(("B", "values", s - VALUES_LAG))
        done = s - VALUES_LAG - 2
        if done >= 0 and done % GROUP == GROUP - 1 and done < heads - 1:
            schedule.append(("B", "unstack", done // GROUP))
        if s == 1:
            schedule.append(("C", "unstack", G - 1))
        if s == 5:
            schedule.append(("A", "turn_x", 0))
        if s == 4:
            schedule.append(("C", "turn_out", 0))
        if s == 7:
            schedule.append(("C", "out", 0))
        if s == 12:
            schedule.append(("N", "normalise", 0))
        for k in range(NP):
            if s == piece_slot[k]:
                schedule.append(("A", "piece", k))
            if s == piece_slot[k] + 1:
                schedule.append(("A", "split", k))
    schedule.append(("A", "v", 0))

    with ExitStack() as ctx:
        m_ = Memory(nc, ctx, name)
        x_in = m_.sb("x_in", [P, 2, TILES, DIM])
        x_res = m_.sb("x_res", [P, 2, TILES, DIM])
        xT = m_.sb("xT", [P, 2, DC, TOK], F32R)
        product = m_.sb("product", [P, len(rotated), 2, TOK])
        turned = m_.sb("turned", [P, len(rotated), TOK])
        parts = m_.sb("parts", [P, NP, 2, TOK], F32R)
        qs = m_.sb("qs", [P, 2, heads, TOK], F32R)
        ks = m_.sb("ks", [P, 2, kv_heads, TOK], F32R)
        v = m_.sb("v", [P, 2, TILES, kv_heads, QUAD])
        probs = m_.sb("probs", [P, PROBS, TILES, TOK])
        neg_max = m_.sb("neg_max", [P, TILES, P])
        max_row = m_.sb("max_row", [P, TOK], F32R)
        stackedO = m_.sb("stackedO", [P, G, 2, TOK])
        inv_sum = m_.sb("inv_sum", [P, G, TILES, GROUP])
        o = m_.sb("o", [P, TILES, DIM])
        oT = m_.sb("oT", [P, 2, DC, TOK], F32R)
        if latent is not None:
            lat = m_.sb("lat", [P, 2, TOK], F32R)
        norm = Norm(m_, consts)

        pT = m_.ps("pT", [P, 4, P])
        pS = [m_.ps(f"pS{i}", [P, TILES, TOK]) for i in range(2)]
        pST = [m_.ps(f"pST{i}", [P, TILES, TOK]) for i in range(2)]
        pW = [m_.ps(f"pW{i}", [P, 2, TOK]) for i in range(3)]

        x_loaded, res_loaded = [m_.sem("x_loaded0"), m_.sem("x_loaded1")], [m_.sem("res_loaded0"), m_.sem("res_loaded1")]
        stacked = [[m_.sem(f"piece{k}_stacked{par}") for par in range(2)] for k in range(NP)]
        max_stacked = [m_.sem("max_stacked0"), m_.sem("max_stacked1")]
        cleared, set_up, res_biased = m_.sem("cleared"), m_.sem("set_up"), m_.sem("res_biased")
        x_turned, xT_hi, xT_lo = m_.sem("x_turned"), m_.sem("xT_hi"), m_.sem("xT_lo")
        latent_ready, latent_hi, latent_lo = m_.sem("latent_ready"), m_.sem("latent_hi"), m_.sem("latent_lo")
        piece_ready, product_ready, turned_ready = m_.sem("piece_ready"), m_.sem("product_ready"), m_.sem("turned_ready")
        turned_hi, turned_lo = m_.sem("turned_hi"), m_.sem("turned_lo")
        plain_hi, plain_lo = m_.sem("plain_hi"), m_.sem("plain_lo")
        v_ready, v_copied = m_.sem("v_ready"), m_.sem("v_copied")
        scores_ready, max_ready, max_turned, max_row_ready = m_.sem("scores_ready"), m_.sem("max_ready"), m_.sem("max_turned"), m_.sem("max_row_ready")
        scoresT_ready, probs_ready, values_done = m_.sem("scoresT_ready"), m_.sem("probs_ready"), m_.sem("values_done")
        group_copied, unstacked, inverted, o_ready = m_.sem("group_copied"), m_.sem("unstacked"), m_.sem("inverted"), m_.sem("o_ready")
        o_turned, oT_hi, oT_lo, out_ready = m_.sem("o_turned"), m_.sem("oT_hi"), m_.sem("oT_lo"), m_.sem("out_ready")

        emptied = {("turn_x", 0): (xT_lo, 1, 1), ("turn_max", 0): (max_row_ready, 1, 1), ("turn_out", 0): (oT_lo, 1, 1),
                   ("latent", 0): (latent_lo, 1, 1), ("v", 0): (v_copied, 1, 1), ("out", 0): (norm.z_ready, 1, 1)}
        for g in range(G):
            emptied["unstack", g] = (o_ready, G, g + 1)
            emptied["values", GROUP * g] = (group_copied, G, g + 1)
        for k in range(NP):
            emptied["piece", k] = ((product_ready, len(rotated), rotated.index(k) + 1) if k in rotated
                                   else (plain_lo, len(plain), plain.index(k) + 1))
        users = {"T": [e for e in schedule if e[1] in ("turn_x", "unstack", "turn_max", "turn_out")]}
        working = [e for e in schedule if e[1] in ("latent", "piece", "v", "out") or e[1] == "values" and e[2] % GROUP == 0]
        bank_of = {e[1:]: n % 3 for n, e in enumerate(working)}
        for n in range(3):
            users[n] = working[n::3]

        def bank_free(pe, i, step):
            using = next(u for u in users.values() if step in [e[1:] for e in u])
            at, body = [e[1:] for e in using].index(step), i
            for _ in using:
                at, body = (at - 1, body) if at else (len(using) - 1, body - 1)
                stage, *before = using[at]
                if sequence_of(stage, body) is not None:
                    sem, per, count = emptied[tuple(before)]
                    return wait(pe, sem, per, sequence_of(stage, body), count)

        block = ctx.enter_context(nc.Block())

        @block.sync
        def _(sp):
            def load_x(b, par):
                wait(sp, x_turned, 1, b, -1)
                sp.dma_start(x_in[:, par], x_from(b)).then_inc(x_loaded[par], 16)

            def load_res(b, par):
                wait(sp, norm.z_ready, 1, b, -1)
                sp.dma_start(x_res[:, par], x_from(b)).then_inc(res_loaded[par], 16)

            def stack(b, par, k):
                p = pieces[k]
                if k in rotated:
                    wait(sp, turned_lo, len(rotated), b, rotated.index(k) + 1)
                else:
                    wait(sp, plain_lo, len(plain), b, plain.index(k) + 1)
                to, order = (qs, (HI, LO, HI)) if p.target == "q" else (ks, (HI, HI, LO))
                for n, part in enumerate(order):
                    row = n * head_dims + p.offset
                    sp.dma_start(f32(to[row:row + p.dims, par, p.first_head:p.first_head + p.heads]),
                                 f32(parts[0:p.dims * p.heads, k, part])).then_inc(stacked[k][par], 16)

            def stack_max(b, par):
                sp.wait_ge(max_row_ready, b + 1)
                sp.dma_start(f32(qs[GUARD_ROW:GUARD_ROW + 1, par]), f32(max_row[0:heads])).then_inc(max_stacked[par], 16)

            def body(i, ip):
                if sequence_of("A", i) is not None:
                    load_x(i + 1, 1 - ip)
                if sequence_of("C", i) is not None:
                    load_res(i - 2, ip)
                for stage, step, k in schedule:
                    b = sequence_of(stage, i)
                    if b is None:
                        continue
                    if step == "split":
                        stack(b, 1 - ip, k)
                    elif step == "turn_max":
                        stack_max(b, ip)
                    elif step == "normalise":
                        norm.store(sp, b, ip, x_to(b))

            sp.wait_ge(set_up, 4)
            over_bodies(sp, body)
            norm.wait_all_stored(sp)

        @block.tensor
        def _(pe):
            def turn_x(b, par):
                pe.wait_ge(x_loaded[par], 8 * (b - par) + 16)
                for c in range(DC):
                    for t in range(TILES):
                        last = pe.transpose(pT[:, 2 * c + t], x_in[:, par, t, c * P:(c + 1) * P], consts["ident"])
                last.then_inc(x_turned, 1)

            def project(out, weights, source):
                moving = [xT[:, part] for part in (HI, LO)] if source == "x" else [lat[:, part:part + 1] for part in (HI, LO)]
                chunks = weights.shape[2]
                for c in range(chunks):
                    for wp, xp in ((HI, HI), (HI, LO), (LO, HI)):
                        last = pe.matmul(out, weights[:, wp, c], moving[xp][:, c], start=c == 0 and wp == xp == HI and project.first,
                                         stop=c == chunks - 1 and wp == LO, skip_group_check=True)
                        project.first = False
                return last

            def latents(b):
                pe.wait_ge(xT_lo, b + 1)
                project.first = True
                project(pW[bank_of["latent", 0]][:, 0], latent["weights"], "x").then_inc(latent_ready, 1)

            def piece(b, k):
                p = pieces[k]
                if p.source == "latent":
                    pe.wait_ge(latent_lo, b + 1)
                elif k == 0:
                    pe.wait_ge(xT_lo, b + 1)
                bank = pW[bank_of["piece", k]]
                project.first = True
                last = project(bank[:, 0], p.plain, p.source)
                if p.swapped is not None:
                    last = project(bank[:, 1], p.swapped, p.source)
                last.then_inc(piece_ready, 1)

            def values_in(b):
                if v_source == "latent":
                    pe.wait_ge(latent_lo, b + 1)
                bank = pW[bank_of["v", 0]]
                chunks = w["v"].shape[2]
                for t in range(TILES):
                    for c in range(chunks):
                        for xp, wp in ((HI, HI), (LO, HI), (HI, LO)):
                            at = xT[:, xp, c] if v_source == "x" else lat[:, xp]
                            last = pe.matmul(bank[:, t, 0:v_features], at[:, t * P:(t + 1) * P], w["v"][:, wp, c],
                                             start=t == 0 and c == 0 and xp == wp == HI,
                                             stop=c == chunks - 1 and wp == LO, skip_group_check=True)
                last.then_inc(v_ready, 1)

            def scores(b, par, h):
                for k, p in enumerate(pieces):
                    if serves_first(p, h):
                        pe.wait_ge(stacked[k][par], 24 * (b - par) + 48)
                wait(pe, max_ready, heads, b, h - 1)
                for t in range(TILES):
                    last = pe.matmul(pS[h % 2][:, t], qs[0:GUARD_ROW, par, h, t * P:(t + 1) * P],
                                     ks[0:GUARD_ROW, par, h // per_kv], start=t == 0, stop=not causal, skip_group_check=True)
                if causal:
                    for t in range(TILES):
                        last = pe.matmul(pS[h % 2][:, t, t * P:(t + 1) * P], consts["ident_bf16"], consts["mask_qk"],
                                         start=False, stop=True, skip_group_check=True)
                last.then_inc(scores_ready, 1)

            def scoresT(b, par, h):
                if h == 0:
                    pe.wait_ge(max_stacked[par], 8 * (b - par) + 16)
                wait(pe, probs_ready, heads, b, h - 1)
                for t in range(TILES):
                    last = pe.matmul(pST[h % 2][:, t], ks[0:GUARD_ROW + 1, par, h // per_kv, t * P:(t + 1) * P],
                                     qs[0:GUARD_ROW + 1, par, h], start=t == 0, stop=not causal, skip_group_check=True)
                if causal:
                    for t in range(TILES):
                        last = pe.matmul(pST[h % 2][:, t, t * P:(t + 1) * P], consts["ident_bf16"], consts["mask_kq"],
                                         start=False, stop=True, skip_group_check=True)
                last.then_inc(scoresT_ready, 1)

            def values(b, par, h):
                g, half, tile = h // GROUP, h % GROUP // 4, h % 4
                bank = pW[bank_of["values", GROUP * g]]
                pe.wait_ge(probs_ready, heads * b + h + 1)
                if h == 0:
                    pe.wait_ge(v_copied, b + 1)
                for t in range(TILES):
                    q0 = t * P if causal else 0
                    last = pe.matmul(bank[QUAD * tile:QUAD * (tile + 1), half, q0:TOK], v[:, par, t, h // per_kv],
                                     probs[:, h % PROBS, t, q0:TOK], start=t == 0, stop=t == TILES - 1,
                                     tile_position=(0, QUAD * tile), skip_group_check=True)
                last.then_inc(values_done, 1)

            def unstack(b, g):
                pe.wait_ge(group_copied, G * b + g + 1)
                for t in range(TILES):
                    for half in range(2):
                        last = pe.transpose(pT[:, 2 * t + half], stackedO[:, g, half, t * P:(t + 1) * P], consts["ident"])
                last.then_inc(unstacked, 1)

            def turn_max(b):
                pe.wait_ge(max_ready, heads * b + heads)
                for t in range(TILES):
                    last = pe.transpose(pT[:, t], neg_max[:, t], consts["ident"])
                last.then_inc(max_turned, 1)

            def turn_out(b):
                pe.wait_ge(o_ready, G * b + G)
                for c in range(DC):
                    for t in range(TILES):
                        last = pe.transpose(pT[:, 2 * c + t], o[:, t, c * P:(c + 1) * P], consts["ident"])
                last.then_inc(o_turned, 1)

            def out(b):
                pe.wait_ge(oT_lo, b + 1)
                bank = pW[bank_of["out", 0]]
                for t in range(TILES):
                    for c in range(DC):
                        for op, wp in ((HI, HI), (LO, HI), (HI, LO)):
                            last = pe.matmul(bank[:, t], oT[:, op, c, t * P:(t + 1) * P], w["out"][:, wp, c],
                                             start=t == 0 and c == 0 and op == wp == HI, stop=c == DC - 1 and wp == LO,
                                             skip_group_check=True)
                last.then_inc(out_ready, 1)

            def body(i, ip):
                for stage, step, k in schedule:
                    b = sequence_of(stage, i)
                    if b is None:
                        continue
                    if (step, k) in emptied:
                        bank_free(pe, i, (step, k))
                    if step == "turn_x":
                        turn_x(b, 1 - ip)
                    elif step == "latent":
                        latents(b)
                    elif step == "piece":
                        piece(b, k)
                    elif step == "v":
                        values_in(b)
                    elif step == "scores":
                        scores(b, ip, k)
                    elif step == "scoresT":
                        scoresT(b, 1 - ip, k)
                    elif step == "values":
                        values(b, 1 - ip, k)
                    elif step == "unstack":
                        unstack(b, k)
                    elif step == "turn_max":
                        turn_max(b)
                    elif step == "turn_out":
                        turn_out(b)
                    elif step == "out":
                        out(b)

            pe.wait_ge(set_up, 4)
            over_bodies(pe, body)

        @block.scalar
        def _(act):
            def body(i, ip):
                for stage, step, k in schedule:
                    b = sequence_of(stage, i)
                    if b is None:
                        continue
                    if step == "turn_x":
                        act.wait_ge(x_turned, b + 1)
                        nc.scalar.copy(xT[:, HI].rearrange("p c q -> p (c q)"), pT[:].rearrange("p a b -> p (a b)")).then_inc(xT_hi, 1)
                    elif step == "latent":
                        act.wait_ge(latent_ready, b + 1)
                        nc.scalar.activation(lat[:, HI], pW[bank_of[step, k]][:, 0], ACT.Identity,
                                             bias=latent["bias"]).then_inc(latent_hi, 1)
                    elif step == "piece" and k in plain:
                        act.wait_ge(piece_ready, NP * b + k + 1)
                        par = 1 - ip
                        wait(act, stacked[k][1 - par], 24, b - 1 - (1 - par), 48)
                        nc.scalar.activation(parts[:, k, HI], pW[bank_of[step, k]][:, 0], ACT.Identity,
                                             bias=pieces[k].bias).then_inc(plain_hi, 1)
                    elif step == "split" and k in rotated:
                        wait(act, turned_ready, len(rotated), b, rotated.index(k) + 1)
                        par = 1 - ip
                        wait(act, stacked[k][1 - par], 24, b - 1 - (1 - par), 48)
                        nc.scalar.copy(parts[:, k, HI], turned[:, rotated.index(k)]).then_inc(turned_hi, 1)
                    elif step == "v" and v_bias is None:
                        act.wait_ge(v_ready, b + 1)
                        nc.scalar.copy(v[:, 1 - ip, :, :, 0:v_dims],
                                       pW[bank_of[step, k]][:, :, 0:v_features].rearrange("p t (h d) -> p t h d", d=v_dims)).then_inc(v_copied, 1)
                    elif step == "scoresT":
                        act.wait_ge(scoresT_ready, heads * b + k + 1)
                        wait(act, values_done, heads, b, k + 1 - PROBS)
                        nc.scalar.activation(probs[:, k % PROBS], pST[k % 2][:], ACT.Exp, scale=scale).then_inc(probs_ready, 1)
                    elif step == "values" and k % GROUP == GROUP - 1:
                        g = k // GROUP
                        act.wait_ge(values_done, heads * b + k + 1)
                        wait(act, unstacked, G, b - 1, g + 1)
                        nc.scalar.copy(stackedO[:, g], pW[bank_of["values", GROUP * g]][:]).then_inc(group_copied, 1)
                    elif step == "turn_max":
                        act.wait_ge(max_turned, b + 1)
                        wait(act, max_stacked[1 - ip], 8, b - 1 - (1 - ip), 16)
                        nc.scalar.copy(max_row[:], pT[:, 0:2].rearrange("p a b -> p (a b)")).then_inc(max_row_ready, 1)
                    elif step == "turn_out":
                        act.wait_ge(o_turned, b + 1)
                        wait(act, out_ready, 1, b, 0)
                        nc.scalar.copy(oT[:, HI].rearrange("p c q -> p (c q)"), pT[:].rearrange("p a b -> p (a b)")).then_inc(oT_hi, 1)

            over_bodies(act, body)

        @block.vector
        def _(dve):
            def rotate(b, k):
                p, r = pieces[k], rotated.index(k)
                bank = pW[bank_of["piece", k]]
                dve.wait_ge(piece_ready, NP * b + k + 1)
                wait(dve, turned_ready, len(rotated), b - 1, r + 1)
                if p.bias is None:
                    dve.tensor_tensor(product[:, r], bank[:], p.table, ALU.mult).then_inc(product_ready, 1)
                else:
                    dve.scalar_tensor_tensor(out=product[:, r, 0], in0=bank[:, 0], scalar=p.bias, in1=p.table[:, 0],
                                             op0=ALU.add, op1=ALU.mult)
                    dve.scalar_tensor_tensor(out=product[:, r, 1], in0=bank[:, 1], scalar=p.swapped_bias, in1=p.table[:, 1],
                                             op0=ALU.add, op1=ALU.mult).then_inc(product_ready, 1)

            def maxima(b, h):
                dve.wait_ge(scores_ready, heads * b + h + 1)
                if h == 0:
                    wait(dve, max_turned, 1, b, 0)
                if causal:
                    dve.tensor_reduce(neg_max[:, 0, h:h + 1], pS[h % 2][:, 0, 0:P], AX.X, ALU.max, negate=True)
                    dve.tensor_reduce(neg_max[:, 1, h:h + 1], pS[h % 2][:, 1], AX.X, ALU.max, negate=True).then_inc(max_ready, 1)
                else:
                    dve.tensor_reduce(neg_max[:, :, h], pS[h % 2][:], AX.X, ALU.max, negate=True).then_inc(max_ready, 1)

            def divide(b, g):
                dve.wait_ge(unstacked, G * b + g + 1)
                wait(dve, o_ready, G, b - 1, g + 1)
                group = pT[:].rearrange("p (t a) (j e) -> p t (a j) e", t=TILES, e=QUAD)
                dve.reciprocal(inv_sum[:, g], group[:, :, :, v_dims]).then_inc(inverted, 1)
                dve.wait_ge(inverted, G * b + g + 1)
                if g == 0:
                    wait(dve, o_turned, 1, b, 0)
                first = GROUP * g * v_dims
                dve.tensor_tensor(o[:, :, first:first + GROUP * v_dims].rearrange("p t (h d) -> p t h d", d=v_dims),
                                  group[:, :, :, 0:v_dims],
                                  inv_sum[:, g].unsqueeze(3).to_broadcast([P, TILES, GROUP, v_dims]),
                                  ALU.mult).then_inc(o_ready, 1)

            def body(i, ip):
                for stage, step, k in schedule:
                    b = sequence_of(stage, i)
                    if b is None:
                        continue
                    if step == "turn_x":
                        dve.wait_ge(xT_hi, b + 1)
                        dve.tensor_tensor(xT[:, LO], pT[:].rearrange("p (c t) q -> p c (t q)", c=DC), f32(xT[:, HI]),
                                          ALU.subtract).then_inc(xT_lo, 1)
                    elif step == "latent":
                        dve.wait_ge(latent_hi, b + 1)
                        dve.scalar_tensor_tensor(out=lat[:, LO], in0=pW[bank_of[step, k]][:, 0], scalar=latent["bias"],
                                                 in1=f32(lat[:, HI]), op0=ALU.add, op1=ALU.subtract).then_inc(latent_lo, 1)
                    elif step == "piece" and k in rotated:
                        rotate(b, k)
                    elif step == "piece":
                        wait(dve, plain_hi, len(plain), b, plain.index(k) + 1)
                        dve.scalar_tensor_tensor(out=parts[:, k, LO], in0=pW[bank_of[step, k]][:, 0], scalar=pieces[k].bias,
                                                 in1=f32(parts[:, k, HI]), op0=ALU.add, op1=ALU.subtract).then_inc(plain_lo, 1)
                    elif step == "v" and v_bias is not None:
                        dve.wait_ge(v_ready, b + 1)
                        for t in range(TILES):
                            last = dve.tensor_tensor(v[:, 1 - ip, t, :, 0:v_dims],
                                                     pW[bank_of[step, k]][:, t, 0:v_features].rearrange("p (h d) -> p h d", d=v_dims),
                                                     v_bias.rearrange("p (h d) -> p h d", d=v_dims), ALU.add)
                        last.then_inc(v_copied, 1)
                    elif step == "scores":
                        maxima(b, k)
                    elif step == "unstack":
                        divide(b, k)
                    elif step == "turn_out":
                        dve.wait_ge(oT_hi, b + 1)
                        dve.tensor_tensor(oT[:, LO], pT[:].rearrange("p (c t) q -> p c (t q)", c=DC), f32(oT[:, HI]),
                                          ALU.subtract).then_inc(oT_lo, 1)
                    elif step == "out":
                        par = ip
                        dve.wait_ge(out_ready, b + 1)
                        if out_bias is None:
                            dve.wait_ge(res_loaded[par], 8 * (b - par) + 16)
                        else:
                            dve.wait_ge(res_biased, b + 1)
                        norm.add_and_measure(dve, b, par, pW[bank_of[step, k]][:], x_res[:, par])
                    elif step == "normalise":
                        norm.normalise(dve, b, ip)

            dve.memset(qs[:].bitcast(F32), 0.0).then_inc(cleared, 1)
            dve.memset(ks[:].bitcast(F32), 0.0).then_inc(cleared, 1)
            dve.memset(v[:], 0.0).then_inc(cleared, 1)
            dve.memset(neg_max[:], 0.0).then_inc(set_up, 1)
            dve.wait_ge(cleared, 3)
            dve.memset(ks[GUARD_ROW:GUARD_ROW + 1].bitcast(F32), 1.0).then_inc(set_up, 1)
            dve.memset(v[:, :, :, :, v_dims:v_dims + 1], 1.0).then_inc(set_up, 2)
            dve.wait_ge(set_up, 4)
            over_bodies(dve, body)

        @block.gpsimd
        def _(pool):
            def body(i, ip):
                for stage, step, k in schedule:
                    b = sequence_of(stage, i)
                    if b is None:
                        continue
                    if step == "piece" and k in rotated:
                        r = rotated.index(k)
                        wait(pool, product_ready, len(rotated), b, r + 1)
                        wait(pool, turned_lo, len(rotated), b - 1, r + 1)
                        pool.tensor_tensor(turned[:, r], product[:, r, 0], product[:, r, 1], ALU.add).then_inc(turned_ready, 1)
                    elif step == "split" and k in rotated:
                        r = rotated.index(k)
                        wait(pool, turned_hi, len(rotated), b, r + 1)
                        pool.tensor_tensor(parts[:, k, LO], turned[:, r], f32(parts[:, k, HI]), ALU.subtract).then_inc(turned_lo, 1)
                    elif step == "turn_out" and out_bias is not None:
                        par = ip
                        pool.wait_ge(res_loaded[par], 8 * (b - par) + 16)
                        for t in range(TILES):
                            last = pool.tensor_tensor(x_res[:, par, t], x_res[:, par, t], out_bias, ALU.add)
                        last.then_inc(res_biased, 1)
                    elif step == "out":
                        norm.invert_root(pool, b, ip)

            over_bodies(pool, body)



PACK = 8
STRIDE = TOK // PACK
UNIT = 2
QUARTER = 64
MASK_ROW = 72
STAGES = {"A": 1, "M": 0, "B": -1, "C": -2}


def staged(stage, i):
    b = i + STAGES[stage]
    return b if not isinstance(b, int) or 0 <= b < SEQS else None


def token_attention_block(nc, name, x_from, x_to, consts, heads, head_dims, v_dims, scale, pieces, w, latent, out_bias,
                          masks):
    assert heads * PACK == P and v_dims * 2 == QUAD and 3 * head_dims <= MASK_ROW
    PACKS, UNITS, ROW = STRIDE, STRIDE // UNIT, heads * TOK
    M_OF_TILE = QUARTER // PACK
    score_pieces = [k for k, p in enumerate(pieces) if p.target != "v"]
    v_pieces = [k for k, p in enumerate(pieces) if p.target == "v"]
    rotated = [k for k in score_pieces if pieces[k].table is not None]
    plain = [k for k in score_pieces if pieces[k].table is None]
    NP, NS, NV = len(pieces), len(score_pieces), len(v_pieces)
    STACK_COUNT = 16 * (3 * NS + NV * (TOK // QUARTER))

    schedule = []
    for s in range(UNITS + VALUES_LAG):
        if s < 2:
            schedule.append(("B", "turn_v", s))
        if s < UNITS:
            schedule.append(("B", "scoresT", s))
        if s >= VALUES_LAG:
            schedule.append(("B", "values", s - VALUES_LAG))
        if s == 3:
            schedule.append(("A", "turn_x", 0))
        if s == 14:
            schedule.append(("C", "divide", 0))
        if s == 5:
            schedule.append(("A", "latent", 0))
        if s >= 6 and s - 6 < NP:
            schedule.append(("A", "piece", s - 6))
        if s >= 7 and s - 7 < NP:
            schedule.append(("A", "split", s - 7))
    for k in range(NP):
        schedule.append(("A", "stack", k))
    for u in range(UNITS):
        if u == 2:
            schedule.append(("C", "out", 0))
        schedule.append(("M", "scores", u))
        if u == 13:
            schedule.append(("C", "normalise", 0))
    schedule.append(("M", "turn_max", 0))

    with ExitStack() as ctx:
        m_ = Memory(nc, ctx, name)
        x_in = m_.sb("x_in", [P, 2, TILES, DIM])
        x_res = m_.sb("x_res", [P, 2, TILES, DIM])
        xT = m_.sb("xT", [P, 2, DC, TOK], F32R)
        lat = m_.sb("lat", [P, 2, TOK], F32R)
        product = m_.sb("product", [P, len(rotated), 2, TOK])
        turned = m_.sb("turned", [P, len(rotated), TOK])
        parts = m_.sb("parts", [P, NS, 2, TOK], F32R)
        v_rows = m_.sb("v_rows", [P, NV, TOK])
        qs = m_.sb("qs", [P, 2, ROW + STRIDE], F32R)
        ks = m_.sb("ks", [P, 2, ROW + STRIDE], F32R)
        vs = m_.sb("vs", [P, 2, heads * QUARTER])
        v = m_.sb("v", [P, M_OF_TILE, P])
        probs = m_.sb("probs", [P, PROBS, UNIT, P])
        neg_max = m_.sb("neg_max", [P, P])
        max_rows = m_.sb("max_rows", [P, P], BF16)
        max_hi = m_.sb("max_hi", [P, P], BF16)
        selected = m_.sb("selected", [P, PACKS])
        pick_pack = m_.sb("pick_pack", [P, PACKS, P], BF16)
        stackedO = m_.sb("stackedO", [P, heads, QUARTER])
        o = m_.sb("o", [P, 2, DC, TOK])
        inv_sum = m_.sb("inv_sum", [P, DC, TOK])
        o32 = m_.sb("o32", [P, DC, TOK])
        oT = m_.sb("oT", [P, 2, DC, TOK], F32R)
        mask_raw = x_in[0:PACK, 0]
        mask_rows = m_.sb("mask_rows", [PACK, 2, TOK], F32R)
        tick, tick_set = m_.sb("tick", [P, 1]), m_.sem("tick_set")
        norm = Norm(m_, consts)

        pT = m_.ps("pT", [P, 4, P])
        pS = m_.ps("pS", [P, UNIT, 2, P])
        pST = [m_.ps(f"pST{i}", [P, UNIT, 2, P]) for i in range(2)]
        score_banks = [pS] + pST
        pW = [m_.ps(f"pW{i}", [P, 2, TOK]) for i in range(2)]
        pO = m_.ps("pO", [P, M_OF_TILE, P])

        x_loaded, res_loaded = [m_.sem("x_loaded0"), m_.sem("x_loaded1")], [m_.sem("res_loaded0"), m_.sem("res_loaded1")]
        stacked = [m_.sem("stacked0"), m_.sem("stacked1")]
        mask_raw_loaded, masks_rounded = m_.sem("mask_raw_loaded"), m_.sem("masks_rounded")
        cleared, set_up, masks_loaded, res_biased = m_.sem("cleared"), m_.sem("set_up"), m_.sem("masks_loaded"), m_.sem("res_biased")
        x_turned, xT_hi, xT_lo = m_.sem("x_turned"), m_.sem("xT_hi"), m_.sem("xT_lo")
        latent_ready, latent_hi, latent_lo = m_.sem("latent_ready"), m_.sem("latent_hi"), m_.sem("latent_lo")
        piece_ready, product_ready, turned_ready = m_.sem("piece_ready"), m_.sem("product_ready"), m_.sem("turned_ready")
        turned_hi, turned_lo = m_.sem("turned_hi"), m_.sem("turned_lo")
        plain_hi, plain_lo, v_taken = m_.sem("plain_hi"), m_.sem("plain_lo"), m_.sem("v_taken")
        v_turned, v_copied = m_.sem("v_turned"), m_.sem("v_copied")
        max_doubled, max_row_hi = m_.sem("max_doubled"), m_.sem("max_row_hi")
        scores_ready, max_ready, max_turned, max_row_ready = m_.sem("scores_ready"), m_.sem("max_ready"), m_.sem("max_turned"), m_.sem("max_row_ready")
        scoresT_ready, probs_ready, values_done = m_.sem("scoresT_ready"), m_.sem("probs_ready"), m_.sem("values_done")
        o_copied, inverted, o_ready = m_.sem("o_copied"), m_.sem("inverted"), m_.sem("o_ready")
        dims_stacked = [m_.sem("dims_stacked0"), m_.sem("dims_stacked1")]
        sums_stacked = [m_.sem("sums_stacked0"), m_.sem("sums_stacked1")]
        oT_hi, oT_lo, out_ready = m_.sem("oT_hi"), m_.sem("oT_lo"), m_.sem("out_ready")
        O_DMAS = DC * (TOK // QUARTER)

        emptied = {("turn_x", 0): (xT_lo, 1, 1), ("turn_max", 0): (max_row_ready, 2, 2), ("turn_v", 0): (v_copied, 2, 1),
                   ("turn_v", 1): (v_copied, 2, 2), ("latent", 0): (latent_lo, 1, 1), ("out", 0): (norm.z_ready, 1, 1)}
        for k in range(NP):
            emptied["piece", k] = ((product_ready, len(rotated), rotated.index(k) + 1) if k in rotated else
                                   (plain_lo, len(plain), plain.index(k) + 1) if k in plain else
                                   (v_taken, NV, v_pieces.index(k) + 1))
        users = {"T": [e for e in schedule if e[1] in ("turn_x", "turn_max", "turn_v")]}
        working = [e for e in schedule if e[1] in ("latent", "piece", "out")]
        bank_of = {e[1:]: n % 2 for n, e in enumerate(working)}
        for n in range(2):
            users[n] = working[n::2]

        def bank_free(pe, i, step):
            using = next(u for u in users.values() if step in [e[1:] for e in u])
            at, body = [e[1:] for e in using].index(step), i
            for _ in using:
                at, body = (at - 1, body) if at else (len(using) - 1, body - 1)
                stage, *before = using[at]
                if staged(stage, body) is not None:
                    sem, per, count = emptied[tuple(before)]
                    return wait(pe, sem, per, staged(stage, body), count)

        block = ctx.enter_context(nc.Block())

        def by_quarter(tokens):
            return tokens.rearrange("p (t q m) -> p q t m", t=PACK, m=M_OF_TILE)

        def by_quarter_order(tokens):
            return tokens.rearrange("p (q t m) -> p q t m", t=PACK, m=M_OF_TILE)

        def run(eng, steps, begin=None):
            def body(i, ip):
                if begin is not None:
                    begin(i, ip)
                for stage, step, k in schedule:
                    b = staged(stage, i)
                    if b is not None and step in steps:
                        steps[step](b, 1 - ip if stage in "AB" else ip, k)
            over_bodies(eng, body, ahead=2)

        def split_done(eng, b, k):
            if k in rotated:
                wait(eng, turned_lo, len(rotated), b, rotated.index(k) + 1)
            else:
                wait(eng, plain_lo, len(plain), b, plain.index(k) + 1)

        def stack_half(eng, par, kind, signal):
            for c in range(DC):
                for q in range(TOK // QUARTER):
                    row = QUAD * q + v_dims * kind
                    eng.dma_start(o[:, kind, c, QUARTER * q:QUARTER * (q + 1)],
                                  stackedO[row:row + v_dims, 8 * c:8 * c + 8]).then_inc(signal[par], 16)

        @block.sync
        def _(sp):
            def stack_dims(b, par, u):
                if u != UNITS - 1:
                    return
                sp.wait_ge(o_copied, 2 * b + 2)
                stack_half(sp, par, 0, dims_stacked)

            def begin(i, ip):
                if isinstance(i, int) and i == -1:
                    sp.dma_start(x_in[:, 0], x_from(0)).then_inc(x_loaded[0], 16)
                if not isinstance(i, int) or i + 2 < SEQS:
                    b, par = i + 2, ip
                    wait(sp, x_turned, 1, b, -1)
                    sp.dma_start(x_in[:, par], x_from(b)).then_inc(x_loaded[par], 16)
                if staged("C", i) is not None:
                    b, par = i - 2, ip
                    wait(sp, norm.z_ready, 1, b, -1)
                    sp.dma_start(x_res[:, par], x_from(b)).then_inc(res_loaded[par], 16)

            def stack(b, par, k):
                p = pieces[k]
                if k == 0:
                    wait(sp, scoresT_ready, UNITS, b, -UNITS)
                    wait(sp, v_turned, 2, b, -2)
                if p.target == "v":
                    wait(sp, v_taken, NV, b, v_pieces.index(k) + 1)
                    for q in range(TOK // QUARTER):
                        sp.dma_start(vs[QUAD * q:QUAD * q + v_dims, par, QUARTER * p.first_head:QUARTER * (p.first_head + p.heads)]
                                     .rearrange("d (h t) -> d h t", t=QUARTER),
                                     v_rows[:, v_pieces.index(k), QUARTER * q:QUARTER * (q + 1)]).then_inc(stacked[par], 16)
                    return
                split_done(sp, b, k)
                to, order = (qs, (HI, LO, HI)) if p.target == "q" else (ks, (HI, HI, LO))
                for n, part in enumerate(order):
                    row = n * head_dims + p.offset
                    sp.dma_start(f32(to[row:row + p.dims, par, TOK * p.first_head:TOK * (p.first_head + p.heads)]).rearrange("d (h t) -> d h t", t=TOK),
                                 f32(parts[0:p.dims * p.heads, score_pieces.index(k), part])).then_inc(stacked[par], 16)

            sp.wait_ge(cleared, 3)
            sp.dma_start(mask_raw, masks).then_inc(mask_raw_loaded, 16)
            sp.wait_ge(masks_rounded, 1)
            for side, to in enumerate((qs, ks)):
                for par in range(2):
                    sp.dma_start(f32(to[MASK_ROW:MASK_ROW + PACK, par, 0:ROW]).rearrange("r (h t) -> r h t", t=TOK),
                                 f32(mask_rows[:, side]).unsqueeze(1).to_broadcast([PACK, heads, TOK])).then_inc(masks_loaded, 16)
            sp.wait_ge(masks_loaded, 64)
            sp.wait_ge(set_up, 1)
            run(sp, {"stack": stack, "values": stack_dims, "normalise": lambda b, par, k: norm.store(sp, b, par, x_to(b))}, begin)
            norm.wait_all_stored(sp)

        @block.tensor
        def _(pe):
            def turn_x(b, par, k):
                pe.wait_ge(x_loaded[par], 8 * (b - par) + 16)
                bank_free(pe, b - STAGES["A"], ("turn_x", 0))
                for c in range(DC):
                    for t in range(TILES):
                        last = pe.transpose(pT[:, 2 * c + t], x_in[:, par, t, c * P:(c + 1) * P], consts["ident"])
                last.then_inc(x_turned, 1)

            def project(bank, side, weights, source):
                chunks = weights.shape[2]
                for c in range(chunks):
                    for wp, xp in ((HI, HI), (HI, LO), (LO, HI)):
                        moving = xT[:, xp, c] if source == "x" else lat[:, xp]
                        last = pe.matmul(bank[:, side], weights[:, wp, c], moving, start=side == 0 and c == 0 and wp == xp == HI,
                                         stop=c == chunks - 1 and wp == LO, skip_group_check=True)
                return last

            def latents(b, par, k):
                pe.wait_ge(xT_lo, b + 1)
                bank_free(pe, b - STAGES["A"], ("latent", 0))
                project(pW[bank_of["latent", 0]], 0, latent["weights"], "x").then_inc(latent_ready, 1)

            def piece(b, par, k):
                p = pieces[k]
                if k == 0 or p.source == "latent":
                    pe.wait_ge(latent_lo, b + 1)
                bank_free(pe, b - STAGES["A"], ("piece", k))
                bank = pW[bank_of["piece", k]]
                last = project(bank, 0, p.plain, p.source)
                if p.swapped is not None:
                    last = project(bank, 1, p.swapped, p.source)
                last.then_inc(piece_ready, 1)

            def pack(rows, par, g):
                return rows[0:GUARD_ROW, par, g:g + STRIDE * (P - 1) + 1:STRIDE]

            def two_packs(rows, par, g):
                return rows[0:GUARD_ROW, par, g:g + ROW].rearrange("r (s n) -> r n s", n=STRIDE)[:, 0:2]

            def scores(b, par, u):
                if u == 0:
                    pe.wait_ge(stacked[par], STACK_COUNT // 2 * (b - par) + STACK_COUNT)
                if u < len(score_banks):
                    wait(pe, probs_ready, UNITS, b, 0)
                    wait(pe, max_ready, UNITS, b, 0)
                else:
                    pe.wait_ge(max_ready, UNITS * b + u + 1 - len(score_banks))
                for n in range(UNIT):
                    last = pe.matmul(score_banks[u % 3][:, n], pack(qs, par, UNIT * u + n), two_packs(ks, par, UNIT * u + n),
                                     start=n == 0, stop=True, skip_group_check=True)
                last.then_inc(scores_ready, 1)

            def scoresT(b, par, u):
                if u == 0:
                    pe.wait_ge(max_row_ready, 2 * b + 2)
                wait(pe, probs_ready, UNITS, b, u - 1)
                for n in range(UNIT):
                    pe.matmul(pST[u % 2][:, n], pack(ks, par, UNIT * u + n), two_packs(qs, par, UNIT * u + n),
                              start=n == 0, stop=False, skip_group_check=True)
                for n in range(UNIT):
                    last = pe.matmul(pST[u % 2][:, n, 0], pick_pack[:, UNIT * u + n], max_rows[:],
                                     start=False, stop=True, skip_group_check=True)
                last.then_inc(scoresT_ready, 1)

            def turn_v(b, par, half):
                bank_free(pe, b - STAGES["B"], ("turn_v", half))
                for n in range(4):
                    at = 4 * half + n
                    last = pe.transpose(pT[:, n], vs[:, par, at:at + M_OF_TILE * (P - 1) + 1:M_OF_TILE], consts["ident"])
                last.then_inc(v_turned, 1)

            def values(b, par, u):
                pe.wait_ge(probs_ready, UNITS * b + u + 1)
                if u == 0:
                    pe.wait_ge(v_copied, 2 * b + 2)
                    wait(pe, o_copied, 2, b, 0)
                for n in range(UNIT):
                    tile, pack = divmod(UNIT * u + n, M_OF_TILE)
                    last = pe.matmul(pO[QUAD * tile:QUAD * (tile + 1), pack], v[:, pack, QUAD * tile:QUAD * (tile + 1)],
                                     probs[:, u % PROBS, n], start=True, stop=True, tile_position=(0, QUAD * tile),
                                     skip_group_check=True)
                last.then_inc(values_done, 1)

            def turn_max(b, par, k):
                pe.wait_ge(max_doubled, b + 1)
                bank_free(pe, b - STAGES["M"], ("turn_max", 0))
                pe.transpose(pT[:, 0], neg_max[:], consts["ident"]).then_inc(max_turned, 1)

            def out(b, par, k):
                pe.wait_ge(oT_lo, b + 1)
                bank_free(pe, b - STAGES["C"], ("out", 0))
                bank = pW[bank_of["out", 0]]
                for t in range(TILES):
                    for c in range(DC):
                        for op, wp in ((HI, HI), (LO, HI), (HI, LO)):
                            last = pe.matmul(bank[:, t], oT[:, op, c, t * P:(t + 1) * P], w["out"][:, wp, c],
                                             start=t == 0 and c == 0 and op == wp == HI, stop=c == DC - 1 and wp == LO,
                                             skip_group_check=True)
                last.then_inc(out_ready, 1)

            pe.wait_ge(set_up, 1)
            pe.wait_ge(masks_loaded, 64)
            run(pe, {"turn_x": turn_x, "latent": latents, "piece": piece, "scores": scores, "scoresT": scoresT,
                     "turn_v": turn_v, "values": values, "turn_max": turn_max, "out": out})

        @block.scalar
        def _(act):
            def turned_x(b, par, k):
                act.wait_ge(x_turned, b + 1)
                nc.scalar.copy(xT[:, HI].rearrange("p c q -> p (c q)"), pT[:].rearrange("p a b -> p (a b)")).then_inc(xT_hi, 1)

            def latents(b, par, k):
                act.wait_ge(latent_ready, b + 1)
                nc.scalar.activation(lat[:, HI], pW[bank_of["latent", 0]][:, 0], ACT.Identity, bias=latent["bias"]).then_inc(latent_hi, 1)

            def previous_stacked(b, par):
                wait(act, stacked[1 - par], STACK_COUNT // 2, b - 1 - (1 - par), STACK_COUNT)

            def piece(b, par, k):
                if k in rotated:
                    return
                act.wait_ge(piece_ready, NP * b + k + 1)
                previous_stacked(b, par)
                bank = pW[bank_of["piece", k]]
                if k in plain:
                    nc.scalar.activation(parts[:, score_pieces.index(k), HI], bank[:, 0], ACT.Identity,
                                         bias=pieces[k].bias).then_inc(plain_hi, 1)
                else:
                    nc.scalar.activation(by_quarter_order(v_rows[:, v_pieces.index(k)]), by_quarter(bank[:, 0]), ACT.Identity,
                                         bias=pieces[k].bias).then_inc(v_taken, 1)

            def split(b, par, k):
                if k not in rotated:
                    return
                wait(act, turned_ready, len(rotated), b, rotated.index(k) + 1)
                previous_stacked(b, par)
                nc.scalar.copy(parts[:, score_pieces.index(k), HI], turned[:, rotated.index(k)]).then_inc(turned_hi, 1)

            def turned_v(b, par, half):
                act.wait_ge(v_turned, 2 * b + half + 1)
                wait(act, values_done, UNITS, b, 0)
                nc.scalar.copy(v[:, 4 * half:4 * half + 4].rearrange("p a b -> p (a b)"),
                               pT[:].rearrange("p a b -> p (a b)")).then_inc(v_copied, 1)

            def exponentials(b, par, u):
                act.wait_ge(scoresT_ready, UNITS * b + u + 1)
                wait(act, values_done, UNITS, b, u + 1 - PROBS)
                nc.scalar.activation(probs[:, u % PROBS], pST[u % 2][:, :, 0], ACT.Exp, scale=scale).then_inc(probs_ready, 1)

            def copy_out(b, par, u):
                if u != UNITS - 1:
                    return
                act.wait_ge(values_done, UNITS * (b + 1))
                for signal in (dims_stacked, sums_stacked):
                    wait(act, signal[1 - par], 8 * O_DMAS, b - 1 - (1 - par), 16 * O_DMAS)
                for half in range(2):
                    packs = slice(4 * half, 4 * half + 4)
                    nc.scalar.copy(stackedO[:].rearrange("p h (t m) -> p m (h t)", t=PACK)[:, packs],
                                   pO[:, packs]).then_inc(o_copied, 1)

            def divided_hi(b, par, k):
                act.wait_ge(o_ready, DC * (b + 1))
                wait(act, out_ready, 1, b, 0)
                nc.scalar.copy(oT[:, HI], o32[:]).then_inc(oT_hi, 1)

            act.wait_ge(mask_raw_loaded, 16)
            nc.scalar.copy(mask_rows[:], mask_raw).then_inc(masks_rounded, 1)
            run(act, {"turn_x": turned_x, "latent": latents, "piece": piece, "split": split, "turn_v": turned_v,
                      "scoresT": exponentials, "values": copy_out, "divide": divided_hi})

        @block.vector
        def _(dve):
            def turned_x(b, par, k):
                dve.wait_ge(xT_hi, b + 1)
                dve.tensor_tensor(xT[:, LO], pT[:].rearrange("p (c t) q -> p c (t q)", c=DC), f32(xT[:, HI]),
                                  ALU.subtract).then_inc(xT_lo, 1)

            def latents(b, par, k):
                dve.wait_ge(latent_hi, b + 1)
                dve.scalar_tensor_tensor(out=lat[:, LO], in0=pW[bank_of["latent", 0]][:, 0], scalar=latent["bias"],
                                         in1=f32(lat[:, HI]), op0=ALU.add, op1=ALU.subtract).then_inc(latent_lo, 1)

            def piece(b, par, k):
                p, bank = pieces[k], pW[bank_of["piece", k]]
                if k in rotated:
                    r = rotated.index(k)
                    dve.wait_ge(piece_ready, NP * b + k + 1)
                    wait(dve, turned_ready, len(rotated), b - 1, r + 1)
                    dve.scalar_tensor_tensor(out=product[:, r, 0], in0=bank[:, 0], scalar=p.bias, in1=p.table[:, 0],
                                             op0=ALU.add, op1=ALU.mult)
                    dve.scalar_tensor_tensor(out=product[:, r, 1], in0=bank[:, 1], scalar=p.swapped_bias, in1=p.table[:, 1],
                                             op0=ALU.add, op1=ALU.mult).then_inc(product_ready, 1)
                elif k in plain:
                    wait(dve, plain_hi, len(plain), b, plain.index(k) + 1)
                    at = score_pieces.index(k)
                    dve.scalar_tensor_tensor(out=parts[:, at, LO], in0=bank[:, 0], scalar=p.bias, in1=f32(parts[:, at, HI]),
                                             op0=ALU.add, op1=ALU.subtract).then_inc(plain_lo, 1)

            def maxima(b, par, u):
                dve.wait_ge(scores_ready, UNITS * b + u + 1)
                if u == 0:
                    wait(dve, max_turned, 1, b, 0)
                dve.tensor_reduce(neg_max[:, UNIT * u:UNIT * (u + 1)], score_banks[u % 3][:, :, 0], AX.X, ALU.max,
                                  negate=True).then_inc(max_ready, 1)
                if u == UNITS - 1:
                    dve.wait_ge(max_ready, UNITS * b + UNITS)
                    dve.tensor_copy(neg_max[:, PACKS:2 * PACKS], neg_max[:, 0:PACKS]).then_inc(max_doubled, 1)

            def turned_max(b, par, k):
                dve.wait_ge(max_turned, b + 1)
                wait(dve, scoresT_ready, UNITS, b, 0)
                dve.tensor_copy(max_hi[:], pT[:, 0]).then_inc(max_row_hi, 1)
                dve.wait_ge(max_row_hi, b + 1)
                dve.tensor_copy(max_rows[0:PACKS], max_hi[0:PACKS]).then_inc(max_row_ready, 1)
                dve.tensor_tensor(max_rows[PACKS:2 * PACKS], pT[PACKS:2 * PACKS, 0], max_hi[PACKS:2 * PACKS],
                                  ALU.subtract).then_inc(max_row_ready, 1)

            def divide(b, par, k):
                for signal in (dims_stacked, sums_stacked):
                    dve.wait_ge(signal[par], 8 * O_DMAS * (b - par) + 16 * O_DMAS)
                wait(dve, oT_lo, 1, b, 0)
                dve.reciprocal(inv_sum[:], o[:, 1]).then_inc(inverted, 1)
                dve.wait_ge(inverted, b + 1)
                for c in range(DC):
                    dve.tensor_tensor(by_quarter(o32[:, c]), by_quarter_order(o[:, 0, c]), by_quarter_order(inv_sum[:, c]),
                                      ALU.mult).then_inc(o_ready, 1)
                dve.wait_ge(oT_hi, b + 1)
                dve.tensor_tensor(oT[:, LO], o32[:], f32(oT[:, HI]), ALU.subtract).then_inc(oT_lo, 1)

            def measure(b, par, k):
                dve.wait_ge(out_ready, b + 1)
                dve.wait_ge(res_biased, b + 1)
                norm.add_and_measure(dve, b, par, pW[bank_of["out", 0]][:], x_res[:, par])

            dve.memset(qs[:].bitcast(F32), 0.0).then_inc(cleared, 1)
            dve.memset(ks[:].bitcast(F32), 0.0).then_inc(cleared, 1)
            dve.memset(vs[:], 1.0).then_inc(cleared, 1)
            dve.memset(neg_max[:], 0.0).then_inc(cleared, 1)
            dve.memset(max_rows[:], 0.0).then_inc(cleared, 1)
            dve.tensor_tensor(selected[:], consts["ident"][:, 0:PACKS], consts["ident"][:, PACKS:2 * PACKS], ALU.add).then_inc(cleared, 1)
            dve.wait_ge(cleared, 6)
            dve.tensor_copy(pick_pack[:], selected[:].unsqueeze(2).to_broadcast([P, PACKS, P])).then_inc(set_up, 1)
            dve.wait_ge(set_up, 1)
            run(dve, {"turn_x": turned_x, "latent": latents, "piece": piece, "scores": maxima, "turn_max": turned_max,
                      "divide": divide, "out": measure, "normalise": lambda b, par, k: norm.normalise(dve, b, par)})

        @block.gpsimd
        def _(pool):
            pool.memset(tick[:], 0.0).then_inc(tick_set, 1)
            pool.wait_ge(tick_set, 1)

            def sum_rotated(b, par, k):
                if k in rotated:
                    r = rotated.index(k)
                    wait(pool, product_ready, len(rotated), b, r + 1)
                    wait(pool, turned_lo, len(rotated), b - 1, r + 1)
                    pool.tensor_tensor(turned[:, r], product[:, r, 0], product[:, r, 1], ALU.add).then_inc(turned_ready, 1)

            def split(b, par, k):
                if k in rotated:
                    r = rotated.index(k)
                    wait(pool, turned_hi, len(rotated), b, r + 1)
                    pool.tensor_tensor(parts[:, score_pieces.index(k), LO], turned[:, r],
                                       f32(parts[:, score_pieces.index(k), HI]), ALU.subtract).then_inc(turned_lo, 1)

            def stack_out(b, par, u):
                if u != UNITS - 1:
                    return
                pool.wait_ge(o_copied, 2 * b + 2)
                wait(pool, o_ready, DC, b, 0)
                pool.tensor_tensor(tick[:], tick[:], tick[:], ALU.add)
                stack_half(pool, par, 1, sums_stacked)

            def bias_residual(b, par, k):
                pool.wait_ge(res_loaded[par], 8 * (b - par) + 16)
                for t in range(TILES):
                    last = pool.tensor_tensor(x_res[:, par, t], x_res[:, par, t], out_bias, ALU.add)
                last.then_inc(res_biased, 1)

            run(pool, {"piece": sum_rotated, "split": split, "values": stack_out, "divide": bias_residual,
                       "out": lambda b, par, k: norm.invert_root(pool, b, par)})



QUARTET = 4
V_COLS = 130
WIDE_PROBS = 4


class Sequence:

    def __init__(self, keys):
        self.off = dict(keys)
        self.keys = keys

    def ordinal(self, key, b):
        body = b + self.off[key]

        def present(at):
            return [k for k, off in self.keys if 0 <= at - off < SEQS]

        if isinstance(body, int):
            before = sum(len(present(at)) for at in range(-1, body))
            return before + present(body).index(key) + 1
        before = len(present(-1)) + len(present(0)) + (body - 1) * len(self.keys)
        return before + [k for k, _ in self.keys].index(key) + 1


def wide_attention_block(nc, name, x_from, x_to, consts, heads, scale, w, bias):
    WD = P
    QUARTETS = heads // QUARTET

    schedule = []
    for g in range(QUARTETS):
        for j in range(QUARTET):
            h = QUARTET * g + j
            schedule.append(("scores", h + QUARTET))
            schedule.append(("scoresT", h))
            schedule.append(("values", h - 1))
            if h == 2:
                schedule.append(("turn_x", heads))
            if h == 4:
                schedule.append(("k", heads))
            if h == 6:
                schedule.append(("v", heads))
            schedule.append(("q", h + 2 * QUARTET))
            if (h - 3) % 2 == 1:
                schedule.append(("turn_out", h - 3))
            if (h - 4) % 2 == 1:
                schedule.append(("out", h - 4))
            if j == QUARTET - 1:
                schedule.append(("turn_max", h + 1))
            if h == 7:
                schedule.append(("normalise", -heads))

    def rolled(b, h):
        return (b + h // heads, h % heads)

    def exists(b):
        return not isinstance(b, int) or 0 <= b < SEQS

    bank_q = Sequence([((step, h % heads), -(h // heads)) for step, h in schedule if step in ("q", "k", "v")])
    bank_t = Sequence([((step, h % heads), -(h // heads)) for step, h in schedule
                       if step in ("turn_x", "turn_max", "turn_out")])

    def over_bodies_wide(eng, body):
        for b in (-1, 0, 1):
            body(b, b % 2)
        with eng.Fori(1, SEQS // 2 - 1) as pair:
            body(2 * pair, 0)
            body(2 * pair + 1, 1)
        for b in (SEQS - 2, SEQS - 1, SEQS, SEQS + 1):
            body(b, b % 2)

    with ExitStack() as ctx:
        m_ = Memory(nc, ctx, name)
        x_in = m_.sb("x_in", [P, 2, TILES, DIM])
        x_res = m_.sb("x_res", [P, 2, TILES, DIM])
        xT = m_.sb("xT", [P, 2, 2, DC, TOK], F32R)
        kT = m_.sb("kT", [P, 2, 2, TOK], F32R)
        qT = m_.sb("qT", [P, 2, heads, TOK], F32R)
        v = m_.sb("v", [P, 2, TILES, V_COLS])
        probs = m_.sb("probs", [P, WIDE_PROBS, TILES, TOK])
        neg_max = m_.sb("neg_max", [P, TILES, P])
        max_row = m_.sb("max_row", [P, 2, TOK], F32R)
        inv_sum = m_.sb("inv_sum", [P, 4, TILES])
        o = m_.sb("o", [P, 4, TILES, WD])
        oT = m_.sb("oT", [P, 2, 2, 2, TOK], F32R)
        norm = Norm(m_, consts)

        pQ = m_.ps("pQ", [P, 2, TOK])
        pT = m_.ps("pT", [P, 4, P])
        pS = m_.ps("pS", [P, TILES, TOK])
        pST = [m_.ps(f"pST{i}", [P, TILES, TOK]) for i in range(2)]
        pV = m_.ps("pV", [P, TILES, TOK])
        pOut = [m_.ps(f"pOut{i}", [P, TILES, DIM]) for i in range(2)]

        x_loaded, res_loaded = [m_.sem("x_loaded0"), m_.sem("x_loaded1")], [m_.sem("res_loaded0"), m_.sem("res_loaded1")]
        set_up, v_cleared, res_biased = m_.sem("set_up"), m_.sem("v_cleared"), m_.sem("res_biased")
        projected, projected_hi = m_.sem("projected"), m_.sem("projected_hi")
        emptied_q, emptied_t = m_.sem("emptied_q"), m_.sem("emptied_t")
        turned, turned_hi = m_.sem("turned"), m_.sem("turned_hi")
        scores_ready, max_ready = m_.sem("scores_ready"), m_.sem("max_ready")
        scoresT_ready, probs_ready, values_done = m_.sem("scoresT_ready"), m_.sem("probs_ready"), m_.sem("values_done")
        inverted, o_ready, out_done = m_.sem("inverted"), m_.sem("o_ready"), m_.sem("out_done")

        hi_q = Sequence([k for k in bank_q.keys if k[0][0] != "v"])
        hi_t = Sequence([k for k in bank_t.keys if k[0][0] != "turn_max"])

        block = ctx.enter_context(nc.Block())

        def run(eng, steps, body_start=None):
            def body(b, par):
                if body_start is not None:
                    body_start(b, par)
                for step, h in schedule:
                    bb, hh = rolled(b, h)
                    if step in steps and exists(bb):
                        steps[step](bb, par if h // heads in (0, -2) else 1 - par, hh)
            over_bodies_wide(eng, body)

        @block.sync
        def _(sp):
            def start(b, par):
                if exists(b + 1):
                    if isinstance(b, int) and b == -1:
                        sp.dma_start(x_in[:, 0], x_from(0)).then_inc(x_loaded[0], 16)
                    if exists(b + 2):
                        wait(sp, emptied_t, 1, bank_t.ordinal(("turn_x", 0), b) if exists(b) else 0, 0)
                        sp.dma_start(x_in[:, par], x_from(b + 2)).then_inc(x_loaded[par], 16)
                if exists(b):
                    wait(sp, norm.z_ready, 1, b, -1)
                    sp.dma_start(x_res[:, par], x_from(b)).then_inc(res_loaded[par], 16)

            run(sp, {"normalise": lambda b, par, h: norm.store(sp, b, par, x_to(b))}, start)
            norm.wait_all_stored(sp)

        @block.tensor
        def _(pe):
            def turn_x(b, par, h):
                pe.wait_ge(x_loaded[par], 8 * (b - par) + 16)
                bank_t_free(("turn_x", 0), b)
                for c in range(DC):
                    for t in range(TILES):
                        last = pe.transpose(pT[:, 2 * c + t], x_in[:, par, t, c * P:(c + 1) * P], consts["ident"])
                last.then_inc(turned, 1)

            def bank_t_free(key, b):
                wait(pe, emptied_t, 1, bank_t.ordinal(key, b), -1)

            def bank_q_free(key, b):
                wait(pe, emptied_q, 1, bank_q.ordinal(key, b), -1)

            def project(out, weights, b, par):
                for c in range(DC):
                    for wp, xp in ((HI, HI), (HI, LO), (LO, HI)):
                        last = pe.matmul(out, weights[:, wp, c], xT[:, par, xp, c], start=c == 0 and wp == xp == HI,
                                         stop=c == DC - 1 and wp == LO)
                return last

            def q(b, par, h):
                bank_q_free(("q", h), b)
                project(pQ[:, 0], w["q"][:, :, :, h * WD:(h + 1) * WD], b, par).then_inc(projected, 1)

            def k(b, par, h):
                pe.wait_ge(emptied_t, bank_t.ordinal(("turn_x", 0), b))
                bank_q_free(("k", 0), b)
                project(pQ[:, 0], w["k"], b, par).then_inc(projected, 1)

            def v_(b, par, h):
                bank_q_free(("v", 0), b)
                for t in range(TILES):
                    for c in range(DC):
                        for xp, wp in ((HI, HI), (LO, HI), (HI, LO)):
                            last = pe.matmul(pQ[:, t], xT[:, par, xp, c, t * P:(t + 1) * P], w["v"][:, wp, c],
                                             start=t == 0 and c == 0 and xp == wp == HI, stop=c == DC - 1 and wp == LO,
                                             skip_group_check=True)
                last.then_inc(projected, 1)

            def scores(b, par, h):
                pe.wait_ge(emptied_q, bank_q.ordinal(("q", h), b))
                wait(pe, max_ready, heads, b, h)
                for t in range(TILES):
                    last = pe.matmul(pS[:, t], qT[:, HI, h, t * P:(t + 1) * P], kT[:, par, HI], start=t == 0, stop=True,
                                     skip_group_check=True)
                last.then_inc(scores_ready, 1)

            def scoresT(b, par, h):
                wait(pe, probs_ready, heads, b, h - 1)
                for t in range(TILES):
                    for kp, qp in ((HI, HI), (HI, LO), (LO, HI)):
                        pe.matmul(pST[h % 2][:, t], kT[:, par, kp, t * P:(t + 1) * P], qT[:, qp, h],
                                  start=t == 0 and kp == qp == HI, stop=False, skip_group_check=True)
                if h % QUARTET == 0:
                    pe.wait_ge(emptied_t, bank_t.ordinal(("turn_max", h), b))
                for t in range(TILES):
                    last = pe.matmul(pST[h % 2][:, t], consts["pick_row"][:, h % QUARTET], max_row[:, h // QUARTET % 2],
                                     start=False, stop=True, skip_group_check=True)
                last.then_inc(scoresT_ready, 1)

            def values(b, par, h):
                pe.wait_ge(probs_ready, heads * b + h + 1)
                if h == 0:
                    pe.wait_ge(emptied_q, bank_q.ordinal(("v", 0), b))
                wait(pe, o_ready, heads, b, h)
                for t in range(TILES):
                    for kt in range(TILES):
                        last = pe.matmul(pV[:, t, 0:V_COLS], probs[:, h % WIDE_PROBS, kt, t * P:(t + 1) * P], v[:, par, kt],
                                         start=t == 0 and kt == 0, stop=kt == TILES - 1, skip_group_check=True)
                last.then_inc(values_done, 1)

            def turn_out(b, par, h):
                pe.wait_ge(o_ready, heads * b + h + 1)
                bank_t_free(("turn_out", h), b)
                for n in range(2):
                    for t in range(TILES):
                        last = pe.transpose(pT[:, 2 * n + t], o[:, (h - 1 + n) % 4, t], consts["ident"])
                last.then_inc(turned, 1)

            def out(b, par, h):
                pe.wait_ge(emptied_t, bank_t.ordinal(("turn_out", h), b))
                if h == 1:
                    wait(pe, norm.z_ready, 1, b, -1)
                for n in range(2):
                    head = h - 1 + n
                    for t in range(TILES):
                        for op, wp in ((HI, HI), (LO, HI), (HI, LO)):
                            last = pe.matmul(pOut[par][:, t], oT[:, op, h // 2 % 2, n, t * P:(t + 1) * P],
                                             w["out"][:, wp, head], start=head == 0 and t == 0 and op == wp == HI,
                                             stop=head == heads - 1 and wp == LO, skip_group_check=True)
                last.then_inc(out_done, 1)

            def turn_max(b, par, h):
                pe.wait_ge(max_ready, heads * b + h + QUARTET)
                bank_t_free(("turn_max", h), b)
                for t in range(TILES):
                    last = pe.transpose(pT[:, t], neg_max[:, t], consts["ident"])
                last.then_inc(turned, 1)

            pe.wait_ge(set_up, 2)
            run(pe, {"turn_x": turn_x, "k": k, "v": v_, "q": q, "scores": scores, "scoresT": scoresT, "values": values,
                     "turn_out": turn_out, "out": out, "turn_max": turn_max})

        @block.scalar
        def _(act):
            def turned_x_hi(b, par, h):
                act.wait_ge(turned, bank_t.ordinal(("turn_x", 0), b))
                nc.scalar.copy(xT[:, par, HI].rearrange("p c q -> p (c q)"), pT[:].rearrange("p a b -> p (a b)")).then_inc(turned_hi, 1)

            def turned_out_hi(b, par, h):
                act.wait_ge(turned, bank_t.ordinal(("turn_out", h), b))
                wait(act, out_done, heads // 2, b, h // 2 - 1)
                nc.scalar.copy(oT[:, HI, h // 2 % 2].rearrange("p n q -> p (n q)"),
                               pT[:].rearrange("p a b -> p (a b)")).then_inc(turned_hi, 1)

            def k_hi(b, par, h):
                act.wait_ge(projected, bank_q.ordinal(("k", 0), b))
                nc.scalar.activation(kT[:, par, HI], pQ[:, 0], ACT.Identity, bias=bias["k"]).then_inc(projected_hi, 1)

            def q_hi(b, par, h):
                act.wait_ge(projected, bank_q.ordinal(("q", h), b))
                wait(act, scoresT_ready, heads, b, h + 1 - heads)
                nc.scalar.activation(qT[:, HI, h], pQ[:, 0], ACT.Identity, bias=bias["q"][:, h:h + 1]).then_inc(projected_hi, 1)

            def exponentials(b, par, h):
                act.wait_ge(scoresT_ready, heads * b + h + 1)
                wait(act, values_done, heads, b, h + 1 - WIDE_PROBS)
                nc.scalar.activation(probs[:, h % WIDE_PROBS], pST[h % 2][:], ACT.Exp, scale=scale).then_inc(probs_ready, 1)

            run(act, {"turn_x": turned_x_hi, "turn_out": turned_out_hi, "k": k_hi, "q": q_hi, "scoresT": exponentials})

        @block.vector
        def _(dve):
            def turned_x_lo(b, par, h):
                dve.wait_ge(turned_hi, hi_t.ordinal(("turn_x", 0), b))
                dve.tensor_tensor(xT[:, par, LO], pT[:].rearrange("p (c t) q -> p c (t q)", c=DC), f32(xT[:, par, HI]),
                                  ALU.subtract).then_inc(emptied_t, 1)

            def turned_out_lo(b, par, h):
                dve.wait_ge(turned_hi, hi_t.ordinal(("turn_out", h), b))
                dve.tensor_tensor(oT[:, LO, h // 2 % 2], pT[:].rearrange("p (n t) q -> p n (t q)", n=2),
                                  f32(oT[:, HI, h // 2 % 2]), ALU.subtract).then_inc(emptied_t, 1)

            def turned_max(b, par, h):
                dve.wait_ge(turned, bank_t.ordinal(("turn_max", h), b))
                wait(dve, scoresT_ready, heads, b, h + QUARTET - 2 * QUARTET)
                dve.tensor_copy(max_row[:, h // QUARTET % 2], pT[:, 0:2].rearrange("p a b -> p (a b)")).then_inc(emptied_t, 1)

            def k_lo(b, par, h):
                dve.wait_ge(projected_hi, hi_q.ordinal(("k", 0), b))
                dve.scalar_tensor_tensor(out=kT[:, par, LO], in0=pQ[:, 0], scalar=bias["k"], in1=f32(kT[:, par, HI]),
                                         op0=ALU.add, op1=ALU.subtract).then_inc(emptied_q, 1)

            def q_lo(b, par, h):
                dve.wait_ge(projected_hi, hi_q.ordinal(("q", h), b))
                dve.scalar_tensor_tensor(out=qT[:, LO, h], in0=pQ[:, 0], scalar=bias["q"][:, h:h + 1],
                                         in1=f32(qT[:, HI, h]), op0=ALU.add, op1=ALU.subtract).then_inc(emptied_q, 1)

            def v_biased(b, par, h):
                dve.wait_ge(projected, bank_q.ordinal(("v", 0), b))
                for t in range(TILES):
                    last = dve.tensor_tensor(v[:, par, t, 0:WD], pQ[:, t, 0:WD], bias["v"], ALU.add)
                last.then_inc(emptied_q, 1)

            def maxima(b, par, h):
                dve.wait_ge(scores_ready, heads * b + h + 1)
                if h % QUARTET == 0:
                    before = (("turn_max", h - QUARTET), b) if h else (("turn_max", heads - QUARTET), b - 1)
                    if exists(before[1]):
                        dve.wait_ge(turned, bank_t.ordinal(*before))
                dve.tensor_reduce(neg_max[:, :, h % QUARTET], pS[:], AX.X, ALU.max, negate=True).then_inc(max_ready, 1)

            def divide(b, par, h):
                dve.wait_ge(values_done, heads * b + h + 1)
                wait(dve, o_ready, heads, b, h - 3)
                dve.reciprocal(inv_sum[:, h % 4], pV[:, :, WD]).then_inc(inverted, 1)
                dve.wait_ge(inverted, heads * b + h + 1)
                if h % 2 == 0:
                    before = (("turn_out", h - 3), b) if h >= 4 else (("turn_out", h - 3 + heads), b - 1)
                    if exists(before[1]):
                        dve.wait_ge(turned, bank_t.ordinal(*before))
                dve.tensor_tensor(o[:, h % 4], pV[:, :, 0:WD], inv_sum[:, h % 4].unsqueeze(2).to_broadcast([P, TILES, WD]),
                                  ALU.mult).then_inc(o_ready, 1)

            def measure(b, par, h):
                if h != heads - 1:
                    return
                dve.wait_ge(out_done, heads // 2 * (b + 1))
                dve.wait_ge(res_biased, b + 1)
                norm.add_and_measure(dve, b, par, pOut[par][:], x_res[:, par])

            dve.memset(v[:], 0.0).then_inc(v_cleared, 1)
            dve.memset(neg_max[:], 0.0).then_inc(set_up, 1)
            dve.wait_ge(v_cleared, 1)
            dve.memset(v[:, :, :, WD:WD + 1], 1.0).then_inc(set_up, 1)
            dve.wait_ge(set_up, 2)
            run(dve, {"turn_x": turned_x_lo, "turn_out": turned_out_lo, "turn_max": turned_max, "k": k_lo, "q": q_lo,
                      "v": v_biased, "scores": maxima, "values": divide, "out": measure,
                      "normalise": lambda b, par, h: norm.normalise(dve, b, par)})

        @block.gpsimd
        def _(pool):
            def add_bias(b, par, h):
                if h == 1:
                    pool.wait_ge(res_loaded[par], 8 * (b - par) + 16)
                    for t in range(TILES):
                        last = pool.tensor_tensor(x_res[:, par, t], x_res[:, par, t], bias["out"], ALU.add)
                    last.then_inc(res_biased, 1)
                if h == heads - 1:
                    norm.invert_root(pool, b, par)

            run(pool, {"out": add_bias})



FFN_HIDDEN = {0: 1024, 1: 1024, 2: 704, 3: 688}
PADDED = {layer: -(-n // P) * P for layer, n in FFN_HIDDEN.items()}
HADAMARD_SCALE = 64.0


def load_constants(nc, m, arrays):
    c = {"ident": m.sb("ident", [P, P])[:], "minus_half": m.sb("minus_half", [P, TILES])[:], "eps": m.sb("eps", [P, TILES])[:],
         "ident_bf16": m.sb("ident_bf16", [P, P], BF16)[:], "mask_qk": m.sb("mask_qk", [P, P], BF16)[:],
         "mask_kq": m.sb("mask_kq", [P, P], BF16)[:], "pick_row": m.sb("pick_row", [P, QUARTET, P], F32R)[:]}
    with ExitStack() as ctx:
        mm = Memory(nc, ctx, "load_constants")
        masks, pick = mm.sb("masks", [P, 3, P]), mm.sb("pick", [P, QUARTET, P])
        loaded, filled, cast = mm.sem("loaded"), mm.sem("filled"), mm.sem("cast")
        block = ctx.enter_context(nc.Block())

        @block.sync
        def _(sp):
            sp.dma_start(masks[:], arrays["masks"]).then_inc(loaded, 16)
            sp.dma_start(c["ident"], arrays["masks"][:, 0]).then_inc(loaded, 16)
            sp.dma_start(pick[:], arrays["pick_row"]).then_inc(loaded, 16)
            sp.wait_ge(loaded, 48)

        @block.gpsimd
        def _(pool):
            pool.memset(c["minus_half"], -0.5).then_inc(filled, 1)
            pool.memset(c["eps"], LN_EPS).then_inc(filled, 1)
            pool.wait_ge(filled, 2)

        @block.vector
        def _(dve):
            dve.wait_ge(loaded, 48)
            for i, n in enumerate(("ident_bf16", "mask_qk", "mask_kq")):
                dve.tensor_copy(c[n], masks[:, i]).then_inc(cast, 1)
            dve.tensor_copy(c["pick_row"], pick[:]).then_inc(cast, 1)
            dve.wait_ge(cast, 4)
    return c


def build(nc, arrays, output, sublayers=range(8)):

    def flat(ap):
        return ap.rearrange("p a b -> p (a b)")

    with ExitStack() as ctx:
        m = Memory(nc, ctx, "all")
        x_all = m.sb("x_all", [P, SEQS, TILES, DIM])
        consts = load_constants(nc, m, arrays)

        def x_of(dram):
            return lambda b: dram[b].rearrange("(t p) d -> p t d", p=P)

        def residual(b):
            return x_all[:, b]

        first, last = sublayers[0], sublayers[-1]

        def run(index, block, *args, **kw):
            x_from = x_of(arrays["x"]) if index == first else residual
            x_to = x_of(output) if index == last else residual
            block(nc, f"s{index}", x_from, x_to, consts, *args, **kw)

        def split(mem, prefix, names, plain=()):
            w = {}
            for n in names:
                chunks, outputs = arrays[f"{prefix}_{n}"].shape[1:]
                w[n] = mem.sb(n, [P, 2, chunks, outputs], F32R)
            kept = {n: mem.sb(n, list(arrays[f"{prefix}_{n}"].shape)) for n in plain}
            split_weights(nc, f"{prefix}_split", [(flat(arrays[f"{prefix}_{n}"]), flat(w[n][:, HI]), flat(w[n][:, LO]), P) for n in names],
                          [(kept[n][:], arrays[f"{prefix}_{n}"]) for n in plain])
            return w, kept

        def load(mem, prefix, names):
            kept = {n: mem.sb(n, list(arrays[f"{prefix}_{n}"].shape)) for n in names}
            split_weights(nc, f"{prefix}_load", [], [(kept[n][:], arrays[f"{prefix}_{n}"]) for n in names])
            return kept

        def ffn_weights(mem, layer, parts):
            M = PADDED[layer] // P
            return {"act": mem.sb("act", [P, parts, DC, PADDED[layer]], F32R), "mul": mem.sb("mul", [P, parts, DC, PADDED[layer]], F32R),
                    "down": mem.sb("down", [P, parts, M, DIM], F32R)}

        def ffn_sources(layer):
            return {n: arrays[f"f{layer}_{n}"] for n in ("act", "mul", "down")}

        if 0 in sublayers:
            with ExitStack() as own:
                mem = Memory(nc, own, "a0")
                w, bias = split(mem, "a0", ("q", "k", "v", "out"), ("q_bias", "k_bias", "v_bias", "out_bias"))
                heads = bias["q_bias"].shape[1]
                run(0, wide_attention_block, heads, float(1 / np.sqrt(np.float32(P))), w,
                    {n: bias[f"{n}_bias"][:] for n in ("q", "k", "v", "out")})
        if 1 in sublayers:
            with ExitStack() as own:
                mem = Memory(nc, own, "f0")
                kept = load(mem, "f0", ("signs_in", "signs_hidden", "act_scale", "mul_scale", "down_scale"))
                w = ffn_weights(mem, 0, 2)
                scaled = scale_hadamard_factors(nc, mem, kept)
                hadamard_fold(nc, "f0_fold", ffn_sources(0), w,
                              {"act": scaled["signs_in"], "mul": scaled["signs_in"], "down": scaled["signs_hidden"]},
                              arrays["hadamard"], scaled["down_scale"])
                run(1, ffn_block, w, ACT.Silu, scaled["act_scale"], scaled["mul_scale"])
        if 2 in sublayers:
            with ExitStack() as own:
                mem = Memory(nc, own, "a1")
                w, kept = split(mem, "a1", ("q", "q_swapped", "k", "k_swapped", "v", "out"), ("rope",))
                heads, dims = 16, 16
                pieces = [Piece(t, GROUP * c, GROUP, dims, 0, "x", w[t][:, :, :, c * P:(c + 1) * P],
                                w[f"{t}_swapped"][:, :, :, c * P:(c + 1) * P], kept["rope"][:]) for c in range(DC) for t in ("q", "k")]
                run(2, small_attention_block, heads, heads, dims, dims, 1 / float(np.sqrt(dims)), pieces, w, causal=True)
        if 3 in sublayers:
            with ExitStack() as own:
                mem = Memory(nc, own, "f1")
                w = ffn_weights(mem, 1, 1)
                scales = {n: mem.sb(f"{n}_scale", [P, 1])[:] for n in w}
                ternary_weights(nc, "f1_quant", ffn_sources(1), w, FFN_HIDDEN[1] * DIM, scales)
                run(3, ffn_block, w, ACT.Silu, scales["act"], scales["mul"], scales["down"])
        if 4 in sublayers:
            with ExitStack() as own:
                mem = Memory(nc, own, "a2")
                w, kept = split(mem, "a2", ("latent", "q", "qr", "qr_swapped", "k", "kr", "kr_swapped", "v", "out"),
                                ("rope", "latent_bias", "q_bias", "k_bias", "qr_bias", "qr_swapped_bias", "kr_bias",
                                 "kr_swapped_bias", "v_bias", "out_bias"))
                heads, dims, rope_dims = 16, 16, 8
                pieces = [Piece(t, GROUP * c, GROUP, dims, 0, "latent", w[t][:, :, :, c * P:(c + 1) * P],
                                bias=kept[f"{t}_bias"][:, c:c + 1]) for t in ("q", "k") for c in range(DC)]
                pieces += [Piece(t, 0, heads, rope_dims, dims, source, w[f"{t}r"][:], w[f"{t}r_swapped"][:], kept["rope"][:],
                                 kept[f"{t}r_bias"][:], kept[f"{t}r_swapped_bias"][:]) for t, source in (("q", "latent"), ("k", "x"))]
                pieces += [Piece("v", GROUP * c, GROUP, dims, 0, "latent", w["v"][:, :, :, c * P:(c + 1) * P],
                                 bias=kept["v_bias"][:, c:c + 1]) for c in range(DC)]
                run(4, token_attention_block, heads, dims + rope_dims, dims, 1 / float(np.sqrt(dims + rope_dims)), pieces, w,
                    {"weights": w["latent"], "bias": kept["latent_bias"][:]}, kept["out_bias"][:], arrays["a2_masks"])
        if 5 in sublayers:
            with ExitStack() as own:
                mem = Memory(nc, own, "f2")
                w = ffn_weights(mem, 2, 1)
                scales = {n: mem.sb(f"{n}_scale", [P, 1])[:] for n in w}
                ternary_weights(nc, "f2_quant", ffn_sources(2), w, FFN_HIDDEN[2] * DIM, scales)
                run(5, ffn_block, w, ACT.Sigmoid)
        if 6 in sublayers:
            with ExitStack() as own:
                mem = Memory(nc, own, "a3")
                w, kept = split(mem, "a3", ("q", "q_swapped", "k", "k_swapped", "v", "out"), ("q_rope", "k_rope"))
                heads, kv_heads, dims = 32, 8, 8
                pieces = [Piece("q", 16 * c, 16, dims, 0, "x", w["q"][:, :, :, c * P:(c + 1) * P],
                                w["q_swapped"][:, :, :, c * P:(c + 1) * P], kept["q_rope"][:]) for c in range(DC)]
                pieces.insert(1, Piece("k", 0, kv_heads, dims, 0, "x", w["k"][:], w["k_swapped"][:], kept["k_rope"][:]))
                run(6, small_attention_block, heads, kv_heads, dims, dims, 1 / float(np.sqrt(dims)), pieces, w)
        if 7 in sublayers:
            with ExitStack() as own:
                mem = Memory(nc, own, "f3")
                w = ffn_weights(mem, 3, 2)
                kept = load(mem, "f3", ("lut",))
                looked_up_weights(nc, "f3_lut", ffn_sources(3), w, kept["lut"], kept["lut"].shape[1])
                run(7, ffn_block, w, ACT.Silu)


def scale_hadamard_factors(nc, mem, kept):
    factors = {"signs_in": 1 / (DIM ** 0.5 * HADAMARD_SCALE), "signs_hidden": 1 / (FFN_HIDDEN[0] ** 0.5 * HADAMARD_SCALE),
               "act_scale": HADAMARD_SCALE, "mul_scale": HADAMARD_SCALE, "down_scale": HADAMARD_SCALE}
    scaled = {n: mem.sb(f"{n}_scaled", list(kept[n].shape)) for n in kept}
    with ExitStack() as ctx:
        done = Memory(nc, ctx, "f0_factors").sem("done")
        block = ctx.enter_context(nc.Block())

        @block.vector
        def _(dve):
            for n, factor in factors.items():
                dve.tensor_scalar(scaled[n][:], kept[n][:], float(factor), None, ALU.mult).then_inc(done, 1)
            dve.wait_ge(done, len(factors))
    return scaled



def chunked(w):
    w = np.pad(w, ((0, -w.shape[0] % P), (0, 0)))
    return np.ascontiguousarray(w.reshape(-1, P, w.shape[1]).transpose(1, 0, 2))


def by_chunk(vector):
    return np.ascontiguousarray(vector.reshape(-1, P).T)


def on_every_partition(vector):
    return np.ascontiguousarray(np.broadcast_to(vector, (P, vector.shape[0])))


def widened(w, columns):
    return np.pad(w, ((0, 0), (0, columns - w.shape[1])))


def dim_major(first_head, heads, dims):
    return ((first_head + np.arange(heads))[None] * dims + np.arange(dims)[:, None]).ravel()


def rope_table(heads, dims, pair_of, negative):
    frequencies = (np.float32(1) / np.float32(10000) ** (np.arange(0, dims, 2, dtype=np.float32) / np.float32(dims))).astype(np.float32)
    angle = (np.arange(TOK, dtype=np.float32)[None] * frequencies[:, None]).astype(np.float32).astype(np.float64)
    dim = np.repeat(np.arange(dims), heads)
    cos, sin = np.cos(angle)[pair_of[dim]], np.sin(angle)[pair_of[dim]] * np.where(negative[dim], -1, 1)[:, None]
    table = np.stack([cos, sin], 1).astype(np.float32)
    return np.pad(table, ((0, P - len(table)), (0, 0), (0, 0)))


def layout(i):
    a = {"x": i["L0_attn_x"]}
    row, col = np.arange(P)[:, None], np.arange(P)[None]
    a["masks"] = np.stack([row == col, np.where(col > row, MASKED, 0), np.where(row > col, MASKED, 0)], 1).astype(np.float32)
    a["pick_row"] = np.ascontiguousarray(np.broadcast_to((np.arange(P)[:, None] == np.arange(QUARTET))[:, :, None], (P, QUARTET, P))).astype(np.float32)
    bits = np.arange(P)[:, None] & np.arange(P)
    parity = sum((bits >> k) & 1 for k in range(7)) % 2
    a["hadamard"] = np.stack([1 - 2 * parity, 2 * parity - 1], 1).astype(np.float32)

    a["a0_q"], a["a0_k"], a["a0_out"] = chunked(i["L0_attn_Wq"]), chunked(i["L0_attn_Wk"]), chunked(i["L0_attn_Wo"])
    a["a0_v"] = chunked(widened(i["L0_attn_Wv"], 2 * P))
    a["a0_q_bias"], a["a0_k_bias"] = by_chunk(i["L0_attn_bq"]), by_chunk(i["L0_attn_bk"])
    a["a0_v_bias"], a["a0_out_bias"] = on_every_partition(i["L0_attn_bv"]), on_every_partition(i["L0_attn_bo"])
    a["f0_act"], a["f0_mul"], a["f0_down"] = chunked(i["L0_ffn_W_gate"].T), chunked(i["L0_ffn_W_up"].T), chunked(i["L0_ffn_W_down"].T)
    a["f0_signs_in"], a["f0_signs_hidden"] = by_chunk(i["L0_ffn_SU_ug"]), by_chunk(i["L0_ffn_SU_dp"])
    hidden = FFN_HIDDEN[0]
    a["f0_mul_scale"], a["f0_act_scale"] = by_chunk(i["L0_ffn_Wscale_ug"][:hidden]), by_chunk(i["L0_ffn_Wscale_ug"][hidden:])
    a["f0_down_scale"] = on_every_partition(i["L0_ffn_Wscale_dp"])

    heads = dims = 16
    order = np.concatenate([dim_major(GROUP * c, GROUP, dims) for c in range(DC)])
    for n, w in zip("qk", (i["L1_attn_Wqkv"][:, :DIM], i["L1_attn_Wqkv"][:, DIM:2 * DIM])):
        a[f"a1_{n}"], a[f"a1_{n}_swapped"] = chunked(w[:, order]), chunked(w[:, order ^ 1])
    a["a1_v"], a["a1_out"] = chunked(i["L1_attn_Wqkv"][:, 2 * DIM:]), chunked(i["L1_attn_Wo"])
    a["a1_rope"] = rope_table(GROUP, dims, np.arange(dims) // 2, np.arange(dims) % 2 == 0)
    a["f1_act"], a["f1_mul"], a["f1_down"] = chunked(i["L1_ffn_W_up"].T), chunked(i["L1_ffn_W_gate"].T), chunked(i["L1_ffn_W_down"].T)

    of_q = lambda w: chunked(np.pad(w, ((0, P - w.shape[0]), (0, 0))))
    of_kv = lambda w: chunked(np.pad(w, ((P - w.shape[0], 0), (0, 0))))
    rope_dims = 8
    rope_order = dim_major(0, heads, rope_dims)
    half = rope_dims // 2
    a["a2_latent"] = chunked(np.concatenate([i["L2_attn_Wc"], i["L2_attn_Wckv"]], 1))
    a["a2_latent_bias"] = by_chunk(np.concatenate([i["L2_attn_bc"], i["L2_attn_bckv"]]))
    a["a2_q"], a["a2_q_bias"] = of_q(i["L2_attn_Wcq"][:, order]), by_chunk(i["L2_attn_bcq"][order])
    a["a2_k"], a["a2_k_bias"] = of_kv(i["L2_attn_Wck"][:, order]), by_chunk(i["L2_attn_bck"][order])
    a["a2_v"], a["a2_v_bias"] = of_kv(i["L2_attn_Wv"][:, order]), by_chunk(i["L2_attn_bv"][order])
    for suffix, at in (("", rope_order), ("_swapped", rope_order ^ half)):
        a[f"a2_qr{suffix}"], a[f"a2_qr{suffix}_bias"] = of_q(i["L2_attn_Wqr"][:, at]), by_chunk(i["L2_attn_bqr"][at])
        a[f"a2_kr{suffix}"], a[f"a2_kr{suffix}_bias"] = chunked(i["L2_attn_Wkr"][:, at]), by_chunk(i["L2_attn_bkr"][at])
    same_token = np.arange(PACK)[:, None] == np.arange(TOK) // STRIDE
    masks = np.stack([same_token, np.where(same_token, 0, MASKED)], 1)
    a["a2_masks"] = masks.astype(np.float32)
    a["a2_out"], a["a2_out_bias"] = chunked(i["L2_attn_Wo"][order]), on_every_partition(i["L2_attn_bo"])
    halves = (np.arange(rope_dims) % half, np.arange(rope_dims) < half)
    a["a2_rope"] = rope_table(heads, rope_dims, *halves)
    a["f2_act"], a["f2_mul"] = (chunked(widened(i[f"L2_ffn_{n}"].T, PADDED[2])) for n in ("w1", "w2"))
    a["f2_down"] = chunked(i["L2_ffn_w3"].T)

    q_order = np.concatenate([dim_major(16 * c, 16, 8) for c in range(DC)])
    k_order = dim_major(0, 8, 8)
    for suffix, swap in (("", 0), ("_swapped", half)):
        a[f"a3_q{suffix}"] = chunked(i["L3_attn_wq"].T[:, q_order ^ swap])
        a[f"a3_k{suffix}"] = chunked(widened(i["L3_attn_wk"].T[:, k_order ^ swap], P))
    a["a3_v"], a["a3_out"] = chunked(i["L3_attn_wv"].T), chunked(i["L3_attn_wo"].T)
    a["a3_q_rope"], a["a3_k_rope"] = rope_table(16, 8, *halves), rope_table(8, 8, *halves)
    lut_size = i["L3_ffn_lut"].shape[0]
    a["f3_lut"] = on_every_partition(i["L3_ffn_lut"])
    pad = PADDED[3] - FFN_HIDDEN[3]
    for n, name in (("act", "gate_idx"), ("mul", "up_idx")):
        a[f"f3_{n}"] = chunked(np.pad(i[f"L3_ffn_{name}"].T, ((0, 0), (0, pad)), constant_values=lut_size))
    a["f3_down"] = chunked(np.pad(i["L3_ffn_down_idx"].T, ((0, pad), (0, 0)), constant_values=lut_size))
    return {n: np.ascontiguousarray(v) for n, v in a.items()}


def kernel(**inputs):
    import concourse.bacc as bacc
    from concourse.bass_utils import run_bass_kernel_spmd

    arrays = layout({n: np.asarray(v) for n, v in inputs.items()})
    nc = bacc.Bacc("TRN2", target_bir_lowering=False, num_devices=1)
    drams = {n: nc.dram_tensor(f"in_{n}", v.shape, I32 if v.dtype.kind == "i" else F32, kind="ExternalInput").ap()
             for n, v in arrays.items()}
    output = nc.dram_tensor("out", (SEQS, TOK, DIM), F32, kind="ExternalOutput").ap()
    build(nc, drams, output)
    result = run_bass_kernel_spmd(nc, [{f"in_{n}": v for n, v in arrays.items()}], core_ids=[0])
    return result.results[0]["out"]
```
